# Optimizing a Trainium2 kernel written in Bass

```python
import numpy as np
import jax
import jax.numpy as jnp

def _softmax(x, axis=-1):
    return jax.nn.softmax(x, axis=axis)

def _gelu(x):
    return jax.nn.gelu(x, approximate=True)

def _silu(x):
    return jax.nn.silu(x)

def _sigmoid(x):
    return jax.nn.sigmoid(x)

def _layernorm(x, axis=-1, eps=1e-05):
    m = jnp.mean(x, axis=axis, keepdims=True)
    v = jnp.var(x, axis=axis, keepdims=True)
    return (x - m) / jnp.sqrt(v + eps)

def _scatter_add(tgt, idx, src, axis=0):
    return tgt.at[idx].add(src)

def _segment_sum(src, seg, n):
    return jax.ops.segment_sum(src, seg, n)
kernel_name = 'mk_decoder_preln_d4_seqx_r8_0f6668'

def setup_inputs(seed: int=0):
    np.random.seed(seed)
    _w = jnp.asarray

    def _rec_inputs():
        import jax
        import jax.numpy as jnp
        _rk = jax.random.key(seed)
        x = 6.313e-05 + 0.9998 * jax.random.normal(jax.random.fold_in(_rk, 1), (64, 64, 128), jnp.float32)
        _lenS = 64 - jax.random.randint(jax.random.fold_in(_rk, 7), (64,), 0, max(1, 64 // 4) + 1, jnp.int32)
        _lenS2 = 64 - jax.random.randint(jax.random.fold_in(_rk, 8), (64,), 0, max(1, 64 // 4) + 1, jnp.int32)
        _ctx_1024P = jax.random.normal(jax.random.fold_in(_rk, 11), (64, 16, 128), jnp.float32)
        _ctx_1024c = jax.random.dirichlet(jax.random.fold_in(_rk, 511), 0.3 * jnp.ones((16,), jnp.float32), (64, 64))
        _ctx_1024t = jnp.einsum('bsk,bkd->bsd', _ctx_1024c, _ctx_1024P)
        _ctx_1024t = _ctx_1024t * jax.lax.rsqrt(jnp.mean(jnp.square(_ctx_1024t)) + 1e-12) * 0.953939
        ctx_1024 = -0.000214406 + 1.00034 * (_ctx_1024t + 0.3 * jax.random.normal(jax.random.fold_in(_rk, 611), (64, 64, 128), jnp.float32))
        return (x, ctx_1024)
    x, ctx_1024 = _rec_inputs()

    def _L0_attn_setup():
        import jax, jax.numpy as jnp
        import numpy as np
        B, N, E, H, DEPTH = (2, 256, 128, 8, 12)
        D = E // H // 2
        LN_EPS = 1e-05
        key = jax.random.key(seed)
        ks = jax.random.split(key, 10)
        w = lambda k: jax.random.normal(k, (E, E), jnp.float32) * E ** (-0.5)
        lp = lambda k: jax.random.normal(k, (D,), jnp.float32) * 0.1
        return {'x': jax.random.normal(ks[0], (B, N, E), jnp.float32), 'Wq': w(ks[1]), 'Wk': w(ks[2]), 'Wv': w(ks[3]), 'Wo': w(ks[4]), 'lq1': lp(ks[5]), 'lk1': lp(ks[6]), 'lq2': lp(ks[7]), 'lk2': lp(ks[8]), 'ln_g': jnp.ones((2 * D,), jnp.float32), 'ln_b': jnp.zeros((2 * D,), jnp.float32)}
    _L0_attn_all = _L0_attn_setup()
    _L0_attn_in = {k: v for k, v in _L0_attn_all.items() if k in ('Wq', 'Wk', 'Wv', 'Wo', 'lq1', 'lk1', 'lq2', 'lk2', 'ln_g', 'ln_b')}
    del _L0_attn_all

    def _L0_xattn_setup():
        import jax, jax.numpy as jnp
        import numpy as np
        from jax import lax
        BIG = jnp.float32(1e+30)

        def _pairwise_euclidean(a, b):
            aa = jnp.sum(a * a, axis=-1)[:, None]
            bb = jnp.sum(b * b, axis=-1)[None, :]
            ab = a @ b.T
            return jnp.sqrt(jnp.maximum(aa + bb - 2.0 * ab, 0.0))

        def _dtw_cost(D):
            row0 = jnp.cumsum(D[0])

            def row_step(prev_row, d_row):
                first = d_row[0] + prev_row[0]

                def col_step(left, inp):
                    d_ij, up, diag = inp
                    r = d_ij + jnp.minimum(jnp.minimum(up, left), diag)
                    return (r, r)
                _, rest = lax.scan(col_step, first, (d_row[1:], prev_row[1:], prev_row[:-1]))
                row = jnp.concatenate([first[None], rest])
                return (row, row)
            _, rows = lax.scan(row_step, row0, D[1:])
            return jnp.concatenate([row0[None], rows], axis=0)

        def _backtrack(R, T1, T2):
            L = T1 + T2 - 1

            def step(carry, _):
                i, j, done = carry
                valid = jnp.logical_not(done)
                cd = jnp.where((i > 0) & (j > 0), R[jnp.maximum(i - 1, 0), jnp.maximum(j - 1, 0)], BIG)
                cu = jnp.where(i > 0, R[jnp.maximum(i - 1, 0), j], BIG)
                cl = jnp.where(j > 0, R[i, jnp.maximum(j - 1, 0)], BIG)
                choice = jnp.argmin(jnp.stack([cd, cu, cl]))
                ni = jnp.where(choice <= 1, i - 1, i)
                nj = jnp.where((choice == 0) | (choice == 2), j - 1, j)
                at_origin = (i == 0) & (j == 0)
                ni = jnp.where(at_origin, 0, ni)
                nj = jnp.where(at_origin, 0, nj)
                return ((ni, nj, done | at_origin), (i, j, valid))
            init = (jnp.int32(T1 - 1), jnp.int32(T2 - 1), jnp.bool_(False))
            _, (i_idx, j_idx, valid) = lax.scan(step, init, None, length=L)
            return (i_idx, j_idx, valid)

        def _align_one(small, large):
            T_small, d = small.shape
            T_large = large.shape[0]
            D = _pairwise_euclidean(small, large)
            R = _dtw_cost(D)
            i_idx, j_idx, valid = _backtrack(R, T_small, T_large)
            contrib = small[i_idx] * valid[:, None].astype(small.dtype)
            expanded = jnp.zeros((T_large, d), dtype=small.dtype).at[j_idx].add(contrib)
            return expanded
        key = jax.random.key(seed)
        k1, k2 = jax.random.split(key)
        teacher = jax.random.normal(k1, (16, 50, 128), dtype=jnp.float32)
        student = jax.random.normal(k2, (16, 75, 128), dtype=jnp.float32)
        return {'teacher_features': teacher, 'student_features': student}
    _L0_xattn_all = _L0_xattn_setup()
    _L0_xattn_in = {k: v for k, v in _L0_xattn_all.items() if k in ()}
    del _L0_xattn_all

    def _L0_ffn_setup():
        import jax, jax.numpy as jnp
        import numpy as np
        LATENT = 128
        LEAF_W = 64
        DEPTH = 4
        N_LEAVES = 2 ** DEPTH
        N_NODES = 2 ** DEPTH - 1
        B, S = (4, 256)

        def _fff_params(key, prefix):
            ks = jax.random.split(key, 4)
            d, h, l, n = (LATENT, LEAF_W, N_LEAVES, N_NODES)
            s_in = 1.0 / np.sqrt(d).astype(np.float32)
            s_h = 1.0 / np.sqrt(h).astype(np.float32)
            return {f'{prefix}_node_w': jax.random.normal(ks[0], (n, d), jnp.float32) * s_in, f'{prefix}_node_b': jax.random.normal(ks[1], (n,), jnp.float32) * s_in, f'{prefix}_w1': jax.random.normal(ks[2], (l, d, h), jnp.float32) * s_in, f'{prefix}_b1': jnp.zeros((l, h), jnp.float32), f'{prefix}_w2': jax.random.normal(ks[3], (l, h, d), jnp.float32) * s_h, f'{prefix}_b2': jnp.zeros((l, d), jnp.float32)}

        def _fff(x, node_w, node_b, w1, b1, w2, b2):
            Bx, Sx, D = x.shape
            xf = x.reshape(-1, D)
            N = xf.shape[0]
            cur = jnp.zeros((N,), jnp.int32)
            for _ in range(DEPTH):
                pw = node_w[cur]
                score = jnp.einsum('nd,nd->n', xf, pw) + node_b[cur]
                cur = 2 * cur + 1 + (score >= 0).astype(jnp.int32)
            leaf = cur - N_NODES
            sel = jax.nn.one_hot(leaf, N_LEAVES, dtype=xf.dtype)
            hidden_all = jax.nn.relu(jnp.einsum('nd,ldh->lnh', xf, w1) + b1[:, None, :])
            hidden = hidden_all * sel.T[:, :, None]
            out = jnp.einsum('lnh,lho->no', hidden, w2) + sel @ b2
            return out.reshape(Bx, Sx, D)
        key = jax.random.key(seed)
        kx, kq, kk, kv = jax.random.split(key, 4)
        inp = {'x': jax.random.normal(kx, (B, S, LATENT), jnp.float32)}
        inp.update(_fff_params(kq, 'q'))
        inp.update(_fff_params(kk, 'k'))
        inp.update(_fff_params(kv, 'v'))
        return inp
    _L0_ffn_all = _L0_ffn_setup()
    _L0_ffn_in = {k: v for k, v in _L0_ffn_all.items() if k in ('q_node_w', 'q_node_b', 'q_w1', 'q_b1', 'q_w2', 'q_b2', 'k_node_w', 'k_node_b', 'k_w1', 'k_b1', 'k_w2', 'k_b2', 'v_node_w', 'v_node_b', 'v_w1', 'v_b1', 'v_w2', 'v_b2')}
    del _L0_ffn_all

    def _L1_attn_setup():
        import jax, jax.numpy as jnp
        import numpy as np
        B, S, E, H = (4, 256, 128, 16)
        HD = E // H
        key = jax.random.key(seed)
        ks = jax.random.split(key, 5)
        scale = 1.0 / np.sqrt(E)
        x = jax.random.normal(ks[0], (B, S, E), dtype=jnp.float32)
        Wqkv = jax.random.uniform(ks[1], (E, 3 * E), dtype=jnp.float32, minval=-scale, maxval=scale)
        bqkv = jax.random.uniform(ks[2], (3 * E,), dtype=jnp.float32, minval=-scale, maxval=scale)
        Wout = jax.random.uniform(ks[3], (E, E), dtype=jnp.float32, minval=-scale, maxval=scale)
        bout = jax.random.uniform(ks[4], (E,), dtype=jnp.float32, minval=-scale, maxval=scale)
        return {'x': x, 'Wqkv': Wqkv, 'bqkv': bqkv, 'Wout': Wout, 'bout': bout}
    _L1_attn_all = _L1_attn_setup()
    _L1_attn_in = {k: v for k, v in _L1_attn_all.items() if k in ('Wqkv', 'bqkv', 'Wout', 'bout')}
    del _L1_attn_all

    def _L1_xattn_setup():
        import jax, jax.numpy as jnp
        import numpy as np
        EPS = 1e-06

        def _rmsnorm(x, w, eps=EPS):
            x32 = x.astype(jnp.float32)
            var = jnp.mean(x32 * x32, axis=-1, keepdims=True)
            return (x32 * jax.lax.rsqrt(var + eps)).astype(x.dtype) * w
        key = jax.random.key(seed)
        ks = jax.random.split(key, 6)
        B, S, K, H = (4, 256, 64, 128)
        return {'hidden_states': jax.random.normal(ks[0], (B, S, H), jnp.float32), 'memory_state': jax.random.normal(ks[1], (B, K, H), jnp.float32), 'q_w': jax.random.normal(ks[2], (H, H), jnp.float32) * (1.0 / np.sqrt(H)), 'k_w': jax.random.normal(ks[3], (H, H), jnp.float32) * (1.0 / np.sqrt(H)), 'norm_w': jnp.ones((H,), jnp.float32), 'gate_w': jax.random.normal(ks[4], (H, H), jnp.float32) * 0.02, 'gate_b': jnp.zeros((H,), jnp.float32)}
    _L1_xattn_all = _L1_xattn_setup()
    _L1_xattn_in = {k: v for k, v in _L1_xattn_all.items() if k in ('q_w', 'k_w', 'norm_w', 'gate_w', 'gate_b')}
    del _L1_xattn_all

    def _L1_ffn_setup():
        import jax, jax.numpy as jnp
        import numpy as np
        TOP_K = 2

        def _mlp(x, w1, b1, w2, b2):
            h = jax.nn.gelu(jnp.einsum('bsd,di->bsi', x, w1) + b1)
            return jnp.einsum('bsi,id->bsd', h, w2) + b2
        key = jax.random.key(seed)
        ks = jax.random.split(key, 8)
        B, S, D, I, E = (2, 256, 128, 512, 8)
        s_in = 1.0 / np.sqrt(D)
        s_mid = 1.0 / np.sqrt(I)
        return {'x': jax.random.normal(ks[0], (B, S, D), jnp.float32), 'gate_w': jax.random.normal(ks[1], (D, E), jnp.float32) * s_in, 'gate_b': jnp.zeros((E,), jnp.float32), 'sh_w1': jax.random.normal(ks[2], (D, I), jnp.float32) * s_in, 'sh_b1': jnp.zeros((I,), jnp.float32), 'sh_w2': jax.random.normal(ks[3], (I, D), jnp.float32) * s_mid, 'sh_b2': jnp.zeros((D,), jnp.float32), 'ew1': jax.random.normal(ks[4], (E, D, I), jnp.float32) * s_in, 'eb1': jnp.zeros((E, I), jnp.float32), 'ew2': jax.random.normal(ks[5], (E, I, D), jnp.float32) * s_mid, 'eb2': jnp.zeros((E, D), jnp.float32)}
    _L1_ffn_all = _L1_ffn_setup()
    _L1_ffn_in = {k: v for k, v in _L1_ffn_all.items() if k in ('gate_w', 'gate_b', 'sh_w1', 'sh_b1', 'sh_w2', 'sh_b2', 'ew1', 'eb1', 'ew2', 'eb2')}
    del _L1_ffn_all

    def _L2_attn_setup():
        import jax, jax.numpy as jnp
        import numpy as np
        D = 128

        def _layernorm(x, gamma, beta, eps=1e-05):
            mu = jnp.mean(x, axis=-1, keepdims=True)
            var = jnp.var(x, axis=-1, keepdims=True)
            return (x - mu) * jax.lax.rsqrt(var + eps) * gamma + beta
        key = jax.random.key(seed)
        ks = jax.random.split(key, 8)
        B, S = (4, 512)
        hidden_states = jax.random.normal(ks[0], (B, S, D), dtype=jnp.float32)
        attention_mask = jnp.ones((B, S), dtype=jnp.int32)
        scale = 0.02
        Wq = jax.random.normal(ks[1], (D, D), jnp.float32) * scale
        bq = jnp.zeros((D,), jnp.float32)
        Wk = jax.random.normal(ks[2], (D, D), jnp.float32) * scale
        bk = jnp.zeros((D,), jnp.float32)
        Wv = jax.random.normal(ks[3], (D, D), jnp.float32) * scale
        bv = jnp.zeros((D,), jnp.float32)
        Wqa = jnp.zeros((D, D), jnp.float32)
        bqa = jnp.ones((D,), jnp.float32)
        Wka = jnp.zeros((D, D), jnp.float32)
        bka = jnp.ones((D,), jnp.float32)
        gamma = jnp.ones((D,), jnp.float32)
        beta = jnp.zeros((D,), jnp.float32)
        return {'hidden_states': hidden_states, 'attention_mask': attention_mask, 'Wq': Wq, 'bq': bq, 'Wqa': Wqa, 'bqa': bqa, 'Wk': Wk, 'bk': bk, 'Wka': Wka, 'bka': bka, 'Wv': Wv, 'bv': bv, 'gamma': gamma, 'beta': beta}
    _L2_attn_all = _L2_attn_setup()
    _L2_attn_in = {k: v for k, v in _L2_attn_all.items() if k in ('attention_mask', 'Wq', 'bq', 'Wqa', 'bqa', 'Wk', 'bk', 'Wka', 'bka', 'Wv', 'bv', 'gamma', 'beta')}
    del _L2_attn_all

    def _L2_xattn_setup():
        import jax, jax.numpy as jnp
        import numpy as np
        D_MODEL = 128
        N_HEADS = 16
        D_K = D_MODEL // N_HEADS

        def _linear(x, w, b):
            return jnp.einsum('bsd,od->bso', x, w) + b
        key = jax.random.key(seed)
        ks = jax.random.split(key, 11)
        B, S, D = (2, 256, D_MODEL)
        scale = 1.0 / np.sqrt(D)
        inp = {'query': jax.random.normal(ks[0], (B, S, D), jnp.float32), 'key': jax.random.normal(ks[1], (B, S, D), jnp.float32), 'value': jax.random.normal(ks[2], (B, S, D), jnp.float32), 'wq': jax.random.normal(ks[3], (D, D), jnp.float32) * scale, 'bq': jax.random.normal(ks[4], (D,), jnp.float32) * scale, 'wk': jax.random.normal(ks[5], (D, D), jnp.float32) * scale, 'bk': jax.random.normal(ks[6], (D,), jnp.float32) * scale, 'wv': jax.random.normal(ks[7], (D, D), jnp.float32) * scale, 'bv': jax.random.normal(ks[8], (D,), jnp.float32) * scale, 'wo': jax.random.normal(ks[9], (D, D), jnp.float32) * scale, 'bo': jax.random.normal(ks[10], (D,), jnp.float32) * scale}
        return inp
    _L2_xattn_all = _L2_xattn_setup()
    _L2_xattn_in = {k: v for k, v in _L2_xattn_all.items() if k in ('wq', 'bq', 'wk', 'bk', 'wv', 'bv', 'wo', 'bo')}
    del _L2_xattn_all

    def _L2_ffn_setup():
        import jax, jax.numpy as jnp
        import numpy as np
        EPS = 1e-05

        def _quantize(W):
            gamma = jnp.mean(jnp.abs(W))
            return jnp.clip(jnp.round(W / (gamma + EPS)), -1.0, 1.0)
        key = jax.random.key(seed)
        k_x, k_w1, k_b1, k_w2, k_b2 = jax.random.split(key, 5)
        n_embd = 128
        d_ff = 4 * n_embd
        B, S = (4, 512)
        bound1 = 1.0 / np.sqrt(n_embd)
        bound2 = 1.0 / np.sqrt(d_ff)
        x = jax.random.normal(k_x, (B, S, n_embd), dtype=jnp.float32)
        W1 = jax.random.uniform(k_w1, (d_ff, n_embd), jnp.float32, -bound1, bound1)
        b1 = jax.random.uniform(k_b1, (d_ff,), jnp.float32, -bound1, bound1)
        W2 = jax.random.uniform(k_w2, (n_embd, d_ff), jnp.float32, -bound2, bound2)
        b2 = jax.random.uniform(k_b2, (n_embd,), jnp.float32, -bound2, bound2)
        return {'x': x, 'W1': W1, 'b1': b1, 'W2': W2, 'b2': b2}
    _L2_ffn_all = _L2_ffn_setup()
    _L2_ffn_in = {k: v for k, v in _L2_ffn_all.items() if k in ('W1', 'b1', 'W2', 'b2')}
    del _L2_ffn_all

    def _L3_attn_setup():
        import jax, jax.numpy as jnp
        import numpy as np
        EMBED_DIM = 128
        NUM_HEADS = 16
        HEAD_DIM = EMBED_DIM // NUM_HEADS
        B, N = (2, 256)
        BIAS_S = 32

        def _interp_matrix(n, s):
            pos = jnp.arange(n, dtype=jnp.float32) * ((s - 1) / (n - 1))
            i0 = jnp.floor(pos).astype(jnp.int32)
            i1 = jnp.minimum(i0 + 1, s - 1)
            frac = pos - i0.astype(jnp.float32)
            rows = jnp.arange(n)
            M = jnp.zeros((n, s), dtype=jnp.float32)
            M = M.at[rows, i0].add(1.0 - frac).at[rows, i1].add(frac)
            return M
        key = jax.random.key(seed)
        ks = jax.random.split(key, 12)
        std = 0.02
        d = {'x': jax.random.normal(ks[0], (B, N, EMBED_DIM), dtype=jnp.float32), 'Wq': jax.random.normal(ks[1], (EMBED_DIM, EMBED_DIM), dtype=jnp.float32) * std, 'bq': jnp.zeros((EMBED_DIM,), dtype=jnp.float32), 'Wk': jax.random.normal(ks[2], (EMBED_DIM, EMBED_DIM), dtype=jnp.float32) * std, 'bk': jnp.zeros((EMBED_DIM,), dtype=jnp.float32), 'Wv': jax.random.normal(ks[3], (EMBED_DIM, EMBED_DIM), dtype=jnp.float32) * std, 'bv': jnp.zeros((EMBED_DIM,), dtype=jnp.float32), 'Wo': jax.random.normal(ks[4], (EMBED_DIM, EMBED_DIM), dtype=jnp.float32) * std, 'bo': jnp.zeros((EMBED_DIM,), dtype=jnp.float32), 'gamma': jnp.ones((EMBED_DIM,), dtype=jnp.float32), 'beta': jnp.zeros((EMBED_DIM,), dtype=jnp.float32), 'rel_bias': jax.random.normal(ks[5], (NUM_HEADS, BIAS_S, BIAS_S), dtype=jnp.float32) * std}
        return d
    _L3_attn_all = _L3_attn_setup()
    _L3_attn_in = {k: v for k, v in _L3_attn_all.items() if k in ('Wq', 'bq', 'Wk', 'bk', 'Wv', 'bv', 'Wo', 'bo', 'gamma', 'beta', 'rel_bias')}
    del _L3_attn_all

    def _L3_xattn_setup():
        import jax, jax.numpy as jnp
        import numpy as np
        import math
        IN_C = 128
        OUT_C = 128
        HEADS = 16
        GROUPS = 4

        def grouped_linear(src, weight, bias):
            g, icg, ocg = weight.shape
            lead = src.shape[:-1]
            s = src.reshape(*lead, g, icg)
            out = jnp.einsum('...gi,gio->...go', s, weight)
            out = out.reshape(*lead, g * ocg)
            return out + bias

        def restricted_softmax(src, margin=0.0):
            src_max = jnp.maximum(jnp.max(src, axis=-1, keepdims=True), 0.0)
            out = jnp.exp(src - src_max)
            return out / (jnp.sum(out, axis=-1, keepdims=True) + jnp.exp(margin - src_max))
        key = jax.random.key(seed)
        ks = jax.random.split(key, 9)
        B, S = (2, 256)
        icg, ocg = (IN_C // GROUPS, OUT_C // GROUPS)
        scale = 1.0 / math.sqrt(icg)
        return {'query': jax.random.normal(ks[0], (B, S, IN_C), jnp.float32), 'key': jax.random.normal(ks[1], (B, S, IN_C), jnp.float32), 'value': jax.random.normal(ks[2], (B, S, IN_C), jnp.float32), 'wq': jax.random.uniform(ks[3], (GROUPS, icg, ocg), jnp.float32, -scale, scale), 'wk': jax.random.uniform(ks[4], (GROUPS, icg, ocg), jnp.float32, -scale, scale), 'wv': jax.random.uniform(ks[5], (GROUPS, icg, ocg), jnp.float32, -scale, scale), 'bq': jax.random.uniform(ks[6], (OUT_C,), jnp.float32, -scale, scale), 'bk': jax.random.uniform(ks[7], (OUT_C,), jnp.float32, -scale, scale), 'bv': jax.random.uniform(ks[8], (OUT_C,), jnp.float32, -scale, scale)}
    _L3_xattn_all = _L3_xattn_setup()
    _L3_xattn_in = {k: v for k, v in _L3_xattn_all.items() if k in ('wq', 'wk', 'wv', 'bq', 'bk', 'bv')}
    del _L3_xattn_all

    def _L3_ffn_setup():
        import jax, jax.numpy as jnp
        import numpy as np
        TOP_K = 2
        CAP_FACTOR = 1.25

        def _gelu(x):
            return 0.5 * x * (1.0 + jnp.tanh(jnp.sqrt(2.0 / jnp.pi) * (x + 0.044715 * x ** 3)))
        key = jax.random.key(seed)
        ks = jax.random.split(key, 6)
        B, S, D, F, E = (4, 256, 128, 512, 8)
        return {'hidden_states': jax.random.normal(ks[0], (B, S, D), dtype=jnp.float32), 'wr': jax.random.normal(ks[1], (E, D), dtype=jnp.float32) * 0.02, 'w1': jax.random.normal(ks[2], (E, D, F), dtype=jnp.float32) * 0.02, 'b1': jnp.zeros((E, F), dtype=jnp.float32), 'w2': jax.random.normal(ks[3], (E, F, D), dtype=jnp.float32) * 0.02, 'b2': jnp.zeros((E, D), dtype=jnp.float32)}
    _L3_ffn_all = _L3_ffn_setup()
    _L3_ffn_in = {k: v for k, v in _L3_ffn_all.items() if k in ('wr', 'w1', 'b1', 'w2', 'b2')}
    del _L3_ffn_all
    return {'x': x, 'ctx_1024': ctx_1024, 'L0_attn_Wq': _L0_attn_in['Wq'], 'L0_attn_Wk': _L0_attn_in['Wk'], 'L0_attn_Wv': _L0_attn_in['Wv'], 'L0_attn_Wo': _L0_attn_in['Wo'], 'L0_attn_lq1': _L0_attn_in['lq1'], 'L0_attn_lk1': _L0_attn_in['lk1'], 'L0_attn_lq2': _L0_attn_in['lq2'], 'L0_attn_lk2': _L0_attn_in['lk2'], 'L0_attn_ln_g': _L0_attn_in['ln_g'], 'L0_attn_ln_b': _L0_attn_in['ln_b'], 'L0_ffn_q_node_w': _L0_ffn_in['q_node_w'], 'L0_ffn_q_node_b': _L0_ffn_in['q_node_b'], 'L0_ffn_q_w1': _L0_ffn_in['q_w1'], 'L0_ffn_q_b1': _L0_ffn_in['q_b1'], 'L0_ffn_q_w2': _L0_ffn_in['q_w2'], 'L0_ffn_q_b2': _L0_ffn_in['q_b2'], 'L0_ffn_k_node_w': _L0_ffn_in['k_node_w'], 'L0_ffn_k_node_b': _L0_ffn_in['k_node_b'], 'L0_ffn_k_w1': _L0_ffn_in['k_w1'], 'L0_ffn_k_b1': _L0_ffn_in['k_b1'], 'L0_ffn_k_w2': _L0_ffn_in['k_w2'], 'L0_ffn_k_b2': _L0_ffn_in['k_b2'], 'L0_ffn_v_node_w': _L0_ffn_in['v_node_w'], 'L0_ffn_v_node_b': _L0_ffn_in['v_node_b'], 'L0_ffn_v_w1': _L0_ffn_in['v_w1'], 'L0_ffn_v_b1': _L0_ffn_in['v_b1'], 'L0_ffn_v_w2': _L0_ffn_in['v_w2'], 'L0_ffn_v_b2': _L0_ffn_in['v_b2'], 'L1_attn_Wqkv': _L1_attn_in['Wqkv'], 'L1_attn_bqkv': _L1_attn_in['bqkv'], 'L1_attn_Wout': _L1_attn_in['Wout'], 'L1_attn_bout': _L1_attn_in['bout'], 'L1_xattn_q_w': _L1_xattn_in['q_w'], 'L1_xattn_k_w': _L1_xattn_in['k_w'], 'L1_xattn_norm_w': _L1_xattn_in['norm_w'], 'L1_xattn_gate_w': _L1_xattn_in['gate_w'], 'L1_xattn_gate_b': _L1_xattn_in['gate_b'], 'L1_ffn_gate_w': _L1_ffn_in['gate_w'], 'L1_ffn_gate_b': _L1_ffn_in['gate_b'], 'L1_ffn_sh_w1': _L1_ffn_in['sh_w1'], 'L1_ffn_sh_b1': _L1_ffn_in['sh_b1'], 'L1_ffn_sh_w2': _L1_ffn_in['sh_w2'], 'L1_ffn_sh_b2': _L1_ffn_in['sh_b2'], 'L1_ffn_ew1': _L1_ffn_in['ew1'], 'L1_ffn_eb1': _L1_ffn_in['eb1'], 'L1_ffn_ew2': _L1_ffn_in['ew2'], 'L1_ffn_eb2': _L1_ffn_in['eb2'], 'L2_attn_attention_mask': _L2_attn_in['attention_mask'], 'L2_attn_Wq': _L2_attn_in['Wq'], 'L2_attn_bq': _L2_attn_in['bq'], 'L2_attn_Wqa': _L2_attn_in['Wqa'], 'L2_attn_bqa': _L2_attn_in['bqa'], 'L2_attn_Wk': _L2_attn_in['Wk'], 'L2_attn_bk': _L2_attn_in['bk'], 'L2_attn_Wka': _L2_attn_in['Wka'], 'L2_attn_bka': _L2_attn_in['bka'], 'L2_attn_Wv': _L2_attn_in['Wv'], 'L2_attn_bv': _L2_attn_in['bv'], 'L2_attn_gamma': _L2_attn_in['gamma'], 'L2_attn_beta': _L2_attn_in['beta'], 'L2_xattn_wq': _L2_xattn_in['wq'], 'L2_xattn_bq': _L2_xattn_in['bq'], 'L2_xattn_wk': _L2_xattn_in['wk'], 'L2_xattn_bk': _L2_xattn_in['bk'], 'L2_xattn_wv': _L2_xattn_in['wv'], 'L2_xattn_bv': _L2_xattn_in['bv'], 'L2_xattn_wo': _L2_xattn_in['wo'], 'L2_xattn_bo': _L2_xattn_in['bo'], 'L2_ffn_W1': _L2_ffn_in['W1'], 'L2_ffn_b1': _L2_ffn_in['b1'], 'L2_ffn_W2': _L2_ffn_in['W2'], 'L2_ffn_b2': _L2_ffn_in['b2'], 'L3_attn_Wq': _L3_attn_in['Wq'], 'L3_attn_bq': _L3_attn_in['bq'], 'L3_attn_Wk': _L3_attn_in['Wk'], 'L3_attn_bk': _L3_attn_in['bk'], 'L3_attn_Wv': _L3_attn_in['Wv'], 'L3_attn_bv': _L3_attn_in['bv'], 'L3_attn_Wo': _L3_attn_in['Wo'], 'L3_attn_bo': _L3_attn_in['bo'], 'L3_attn_gamma': _L3_attn_in['gamma'], 'L3_attn_beta': _L3_attn_in['beta'], 'L3_attn_rel_bias': _L3_attn_in['rel_bias'], 'L3_xattn_wq': _L3_xattn_in['wq'], 'L3_xattn_wk': _L3_xattn_in['wk'], 'L3_xattn_wv': _L3_xattn_in['wv'], 'L3_xattn_bq': _L3_xattn_in['bq'], 'L3_xattn_bk': _L3_xattn_in['bk'], 'L3_xattn_bv': _L3_xattn_in['bv'], 'L3_ffn_wr': _L3_ffn_in['wr'], 'L3_ffn_w1': _L3_ffn_in['w1'], 'L3_ffn_b1': _L3_ffn_in['b1'], 'L3_ffn_w2': _L3_ffn_in['w2'], 'L3_ffn_b2': _L3_ffn_in['b2']}

def reference(x, ctx_1024, L0_attn_Wq, L0_attn_Wk, L0_attn_Wv, L0_attn_Wo, L0_attn_lq1, L0_attn_lk1, L0_attn_lq2, L0_attn_lk2, L0_attn_ln_g, L0_attn_ln_b, L0_ffn_q_node_w, L0_ffn_q_node_b, L0_ffn_q_w1, L0_ffn_q_b1, L0_ffn_q_w2, L0_ffn_q_b2, L0_ffn_k_node_w, L0_ffn_k_node_b, L0_ffn_k_w1, L0_ffn_k_b1, L0_ffn_k_w2, L0_ffn_k_b2, L0_ffn_v_node_w, L0_ffn_v_node_b, L0_ffn_v_w1, L0_ffn_v_b1, L0_ffn_v_w2, L0_ffn_v_b2, L1_attn_Wqkv, L1_attn_bqkv, L1_attn_Wout, L1_attn_bout, L1_xattn_q_w, L1_xattn_k_w, L1_xattn_norm_w, L1_xattn_gate_w, L1_xattn_gate_b, L1_ffn_gate_w, L1_ffn_gate_b, L1_ffn_sh_w1, L1_ffn_sh_b1, L1_ffn_sh_w2, L1_ffn_sh_b2, L1_ffn_ew1, L1_ffn_eb1, L1_ffn_ew2, L1_ffn_eb2, L2_attn_attention_mask, L2_attn_Wq, L2_attn_bq, L2_attn_Wqa, L2_attn_bqa, L2_attn_Wk, L2_attn_bk, L2_attn_Wka, L2_attn_bka, L2_attn_Wv, L2_attn_bv, L2_attn_gamma, L2_attn_beta, L2_xattn_wq, L2_xattn_bq, L2_xattn_wk, L2_xattn_bk, L2_xattn_wv, L2_xattn_bv, L2_xattn_wo, L2_xattn_bo, L2_ffn_W1, L2_ffn_b1, L2_ffn_W2, L2_ffn_b2, L3_attn_Wq, L3_attn_bq, L3_attn_Wk, L3_attn_bk, L3_attn_Wv, L3_attn_bv, L3_attn_Wo, L3_attn_bo, L3_attn_gamma, L3_attn_beta, L3_attn_rel_bias, L3_xattn_wq, L3_xattn_wk, L3_xattn_wv, L3_xattn_bq, L3_xattn_bk, L3_xattn_bv, L3_ffn_wr, L3_ffn_w1, L3_ffn_b1, L3_ffn_w2, L3_ffn_b2):
    import jax
    import jax.numpy as jnp

    def _L0_attn_ref(x, Wq, Wk, Wv, Wo, lq1, lk1, lq2, lk2, ln_g, ln_b):
        import jax, jax.numpy as jnp
        import numpy as np
        B, N, E, H, DEPTH = (2, 256, 128, 8, 12)
        D = E // H // 2
        LN_EPS = 1e-05
        b, n, e = x.shape
        lam_init = 0.8 - 0.6 * np.exp(-0.3 * DEPTH)
        q = (x @ Wq).reshape(b, n, 2 * H, D).transpose(0, 2, 1, 3) * D ** (-0.5)
        k = (x @ Wk).reshape(b, n, 2 * H, D).transpose(0, 2, 1, 3)
        v = (x @ Wv).reshape(b, n, H, 2 * D).transpose(0, 2, 1, 3)
        scores = jnp.einsum('bhqd,bhkd->bhqk', q, k)
        attn = jax.nn.softmax(scores, axis=-1).reshape(b, H, 2, n, n)
        lam = jnp.exp(jnp.sum(lq1 * lk1)) - jnp.exp(jnp.sum(lq2 * lk2)) + lam_init
        w_diff = attn[:, :, 0] - lam * attn[:, :, 1]
        o = jnp.einsum('bhqk,bhkd->bhqd', w_diff, v)
        mu = o.mean(-1, keepdims=True)
        var = ((o - mu) ** 2).mean(-1, keepdims=True)
        o = (o - mu) * jax.lax.rsqrt(var + LN_EPS) * ln_g + ln_b
        o = o.transpose(0, 2, 1, 3).reshape(b, n, e)
        return o @ Wo

    def _L0_xattn_ref(teacher_features, student_features):
        import jax, jax.numpy as jnp
        import numpy as np
        from jax import lax
        BIG = jnp.float32(1e+30)

        def _pairwise_euclidean(a, b):
            aa = jnp.sum(a * a, axis=-1)[:, None]
            bb = jnp.sum(b * b, axis=-1)[None, :]
            ab = a @ b.T
            return jnp.sqrt(jnp.maximum(aa + bb - 2.0 * ab, 0.0))

        def _dtw_cost(D):
            row0 = jnp.cumsum(D[0])

            def row_step(prev_row, d_row):
                first = d_row[0] + prev_row[0]

                def col_step(left, inp):
                    d_ij, up, diag = inp
                    r = d_ij + jnp.minimum(jnp.minimum(up, left), diag)
                    return (r, r)
                _, rest = lax.scan(col_step, first, (d_row[1:], prev_row[1:], prev_row[:-1]))
                row = jnp.concatenate([first[None], rest])
                return (row, row)
            _, rows = lax.scan(row_step, row0, D[1:])
            return jnp.concatenate([row0[None], rows], axis=0)

        def _backtrack(R, T1, T2):
            L = T1 + T2 - 1

            def step(carry, _):
                i, j, done = carry
                valid = jnp.logical_not(done)
                cd = jnp.where((i > 0) & (j > 0), R[jnp.maximum(i - 1, 0), jnp.maximum(j - 1, 0)], BIG)
                cu = jnp.where(i > 0, R[jnp.maximum(i - 1, 0), j], BIG)
                cl = jnp.where(j > 0, R[i, jnp.maximum(j - 1, 0)], BIG)
                choice = jnp.argmin(jnp.stack([cd, cu, cl]))
                ni = jnp.where(choice <= 1, i - 1, i)
                nj = jnp.where((choice == 0) | (choice == 2), j - 1, j)
                at_origin = (i == 0) & (j == 0)
                ni = jnp.where(at_origin, 0, ni)
                nj = jnp.where(at_origin, 0, nj)
                return ((ni, nj, done | at_origin), (i, j, valid))
            init = (jnp.int32(T1 - 1), jnp.int32(T2 - 1), jnp.bool_(False))
            _, (i_idx, j_idx, valid) = lax.scan(step, init, None, length=L)
            return (i_idx, j_idx, valid)

        def _align_one(small, large):
            T_small, d = small.shape
            T_large = large.shape[0]
            D = _pairwise_euclidean(small, large)
            R = _dtw_cost(D)
            i_idx, j_idx, valid = _backtrack(R, T_small, T_large)
            contrib = small[i_idx] * valid[:, None].astype(small.dtype)
            expanded = jnp.zeros((T_large, d), dtype=small.dtype).at[j_idx].add(contrib)
            return expanded
        return jax.vmap(_align_one)(teacher_features, student_features)

    def _L0_ffn_ref(x, q_node_w, q_node_b, q_w1, q_b1, q_w2, q_b2, k_node_w, k_node_b, k_w1, k_b1, k_w2, k_b2, v_node_w, v_node_b, v_w1, v_b1, v_w2, v_b2):
        import jax, jax.numpy as jnp
        import numpy as np
        LATENT = 128
        LEAF_W = 64
        DEPTH = 4
        N_LEAVES = 2 ** DEPTH
        N_NODES = 2 ** DEPTH - 1
        B, S = (4, 256)

        def _fff_params(key, prefix):
            ks = jax.random.split(key, 4)
            d, h, l, n = (LATENT, LEAF_W, N_LEAVES, N_NODES)
            s_in = 1.0 / np.sqrt(d).astype(np.float32)
            s_h = 1.0 / np.sqrt(h).astype(np.float32)
            return {f'{prefix}_node_w': jax.random.normal(ks[0], (n, d), jnp.float32) * s_in, f'{prefix}_node_b': jax.random.normal(ks[1], (n,), jnp.float32) * s_in, f'{prefix}_w1': jax.random.normal(ks[2], (l, d, h), jnp.float32) * s_in, f'{prefix}_b1': jnp.zeros((l, h), jnp.float32), f'{prefix}_w2': jax.random.normal(ks[3], (l, h, d), jnp.float32) * s_h, f'{prefix}_b2': jnp.zeros((l, d), jnp.float32)}

        def _fff(x, node_w, node_b, w1, b1, w2, b2):
            Bx, Sx, D = x.shape
            xf = x.reshape(-1, D)
            N = xf.shape[0]
            cur = jnp.zeros((N,), jnp.int32)
            for _ in range(DEPTH):
                pw = node_w[cur]
                score = jnp.einsum('nd,nd->n', xf, pw) + node_b[cur]
                cur = 2 * cur + 1 + (score >= 0).astype(jnp.int32)
            leaf = cur - N_NODES
            sel = jax.nn.one_hot(leaf, N_LEAVES, dtype=xf.dtype)
            hidden_all = jax.nn.relu(jnp.einsum('nd,ldh->lnh', xf, w1) + b1[:, None, :])
            hidden = hidden_all * sel.T[:, :, None]
            out = jnp.einsum('lnh,lho->no', hidden, w2) + sel @ b2
            return out.reshape(Bx, Sx, D)
        q = _fff(x, q_node_w, q_node_b, q_w1, q_b1, q_w2, q_b2)
        k = _fff(x, k_node_w, k_node_b, k_w1, k_b1, k_w2, k_b2)
        v = _fff(x, v_node_w, v_node_b, v_w1, v_b1, v_w2, v_b2)
        scale = 1.0 / np.sqrt(LATENT).astype(np.float32)
        attn = jax.nn.softmax(jnp.einsum('bqd,bkd->bqk', q, k) * scale, axis=-1)
        return jnp.einsum('bqk,bkd->bqd', attn, v)

    def _L1_attn_ref(x, Wqkv, bqkv, Wout, bout):
        import jax, jax.numpy as jnp
        import numpy as np
        B, S, E, H = (4, 256, 128, 16)
        HD = E // H
        b, s, e = x.shape
        qkv = x @ Wqkv + bqkv
        qkv = qkv.reshape(b, s, H, 3 * HD)
        q, k, v = (qkv[..., :HD], qkv[..., HD:2 * HD], qkv[..., 2 * HD:])
        scores = jnp.einsum('bqhd,bkhd->bhqk', q, k) / jnp.sqrt(jnp.float32(HD))
        attn = jax.nn.softmax(scores, axis=-1)
        out = jnp.einsum('bhqk,bkhd->bqhd', attn, v).reshape(b, s, e)
        return out @ Wout + bout

    def _L1_xattn_ref(hidden_states, memory_state, q_w, k_w, norm_w, gate_w, gate_b):
        import jax, jax.numpy as jnp
        import numpy as np
        EPS = 1e-06

        def _rmsnorm(x, w, eps=EPS):
            x32 = x.astype(jnp.float32)
            var = jnp.mean(x32 * x32, axis=-1, keepdims=True)
            return (x32 * jax.lax.rsqrt(var + eps)).astype(x.dtype) * w
        B, S, H = hidden_states.shape
        K = memory_state.shape[1]
        scale = 1.0 / np.sqrt(H)
        normed = _rmsnorm(hidden_states, norm_w)
        v_pool = jnp.concatenate([normed, memory_state], axis=1)
        q = jnp.einsum('bsh,oh->bso', normed, q_w)
        k = jnp.einsum('bth,oh->bto', v_pool, k_w)
        logits = jnp.einsum('bsd,btd->bst', q, k) * scale
        local = jnp.tril(jnp.ones((S, S), bool))
        mask = jnp.concatenate([local, jnp.ones((S, K), bool)], axis=1)
        logits = jnp.where(mask[None], logits, -jnp.inf)
        attn = jax.nn.softmax(logits, axis=-1)
        h_tilde = jnp.einsum('bst,bth->bsh', attn, v_pool)
        alpha = jax.nn.sigmoid(jnp.einsum('bsh,oh->bso', hidden_states, gate_w) + gate_b)
        return (1.0 - alpha) * hidden_states + alpha * h_tilde

    def _L1_ffn_ref(x, gate_w, gate_b, sh_w1, sh_b1, sh_w2, sh_b2, ew1, eb1, ew2, eb2):
        import jax, jax.numpy as jnp
        import numpy as np
        TOP_K = 2

        def _mlp(x, w1, b1, w2, b2):
            h = jax.nn.gelu(jnp.einsum('bsd,di->bsi', x, w1) + b1)
            return jnp.einsum('bsi,id->bsd', h, w2) + b2
        E = ew1.shape[0]
        router_probs = jax.nn.softmax(jnp.einsum('bsd,de->bse', x, gate_w) + gate_b, axis=-1)
        expert_values, expert_indices = jax.lax.top_k(router_probs, k=TOP_K)
        expert_values = expert_values / (jnp.sum(expert_values, axis=-1, keepdims=True) + 1e-09)
        h = jax.nn.gelu(jnp.einsum('bsd,edi->bsei', x, ew1) + eb1)
        all_outputs = jnp.einsum('bsei,eid->bsed', h, ew2) + eb2
        one_hot = jax.nn.one_hot(expert_indices, E, dtype=x.dtype)
        weights_E = (one_hot * expert_values[..., None]).sum(axis=2)
        moe_out = jnp.einsum('bse,bsed->bsd', weights_E, all_outputs)
        return x + _mlp(x, sh_w1, sh_b1, sh_w2, sh_b2) + moe_out

    def _L2_attn_ref(hidden_states, attention_mask, Wq, bq, Wqa, bqa, Wk, bk, Wka, bka, Wv, bv, gamma, beta):
        import jax, jax.numpy as jnp
        import numpy as np
        D = 128

        def _layernorm(x, gamma, beta, eps=1e-05):
            mu = jnp.mean(x, axis=-1, keepdims=True)
            var = jnp.var(x, axis=-1, keepdims=True)
            return (x - mu) * jax.lax.rsqrt(var + eps) * gamma + beta
        h = _layernorm(hidden_states, gamma, beta)
        B, S, d_model = h.shape
        inv_sqrt_d = 1.0 / jnp.sqrt(jnp.float32(d_model))
        query = h @ Wq + bq
        keys = h @ Wk + bk
        values = h @ Wv + bv
        scaling = jnp.arange(1, S + 1, dtype=h.dtype).reshape(1, S, 1)
        query_weight = jax.nn.softmax((query @ Wqa + bqa) * inv_sqrt_d, axis=-1)
        pooled_query = jnp.cumsum(query_weight * query, axis=1) / scaling
        mixed_keys = pooled_query * keys
        keys_weight = jax.nn.softmax((mixed_keys @ Wka + bka) * inv_sqrt_d, axis=-1)
        pooled_keys = jnp.cumsum(keys_weight * mixed_keys, axis=1) / scaling
        return pooled_keys * values

    def _L2_xattn_ref(query, key, value, wq, bq, wk, bk, wv, bv, wo, bo):
        import jax, jax.numpy as jnp
        import numpy as np
        D_MODEL = 128
        N_HEADS = 16
        D_K = D_MODEL // N_HEADS

        def _linear(x, w, b):
            return jnp.einsum('bsd,od->bso', x, w) + b
        B, S, D = query.shape
        H, Dk = (N_HEADS, D_K)
        q = _linear(query, wq, bq).reshape(B, S, H, Dk).transpose(0, 2, 1, 3)
        k = _linear(key, wk, bk).reshape(B, S, H, Dk).transpose(0, 2, 1, 3)
        v = _linear(value, wv, bv).reshape(B, S, H, Dk).transpose(0, 2, 1, 3)
        scores = jnp.einsum('bhqd,bhkd->bhqk', q, k) / jnp.sqrt(jnp.float32(Dk))
        attn = jax.nn.softmax(scores, axis=-1)
        ctx = jnp.einsum('bhqk,bhkd->bhqd', attn, v)
        ctx = ctx.transpose(0, 2, 1, 3).reshape(B, S, D)
        return _linear(ctx, wo, bo)

    def _L2_ffn_ref(x, W1, b1, W2, b2):
        import jax, jax.numpy as jnp
        import numpy as np
        EPS = 1e-05

        def _quantize(W):
            gamma = jnp.mean(jnp.abs(W))
            return jnp.clip(jnp.round(W / (gamma + EPS)), -1.0, 1.0)
        Wq1 = _quantize(W1)
        Wq2 = _quantize(W2)
        h = jax.nn.relu(jnp.einsum('bsd,fd->bsf', x, Wq1) + b1)
        out = jnp.einsum('bsf,df->bsd', h, Wq2) + b2
        return out

    def _L3_attn_ref(x, Wq, bq, Wk, bk, Wv, bv, Wo, bo, gamma, beta, rel_bias):
        import jax, jax.numpy as jnp
        import numpy as np
        EMBED_DIM = 128
        NUM_HEADS = 16
        HEAD_DIM = EMBED_DIM // NUM_HEADS
        B, N = (2, 256)
        BIAS_S = 32

        def _interp_matrix(n, s):
            pos = jnp.arange(n, dtype=jnp.float32) * ((s - 1) / (n - 1))
            i0 = jnp.floor(pos).astype(jnp.int32)
            i1 = jnp.minimum(i0 + 1, s - 1)
            frac = pos - i0.astype(jnp.float32)
            rows = jnp.arange(n)
            M = jnp.zeros((n, s), dtype=jnp.float32)
            M = M.at[rows, i0].add(1.0 - frac).at[rows, i1].add(frac)
            return M
        Bx, Nx, C = x.shape
        H, D = (NUM_HEADS, HEAD_DIM)
        scale = 1.0 / jnp.sqrt(jnp.float32(D))
        mu = jnp.mean(x, axis=-1, keepdims=True)
        var = jnp.mean(jnp.square(x - mu), axis=-1, keepdims=True)
        xn = (x - mu) * jax.lax.rsqrt(var + 1e-05) * gamma + beta
        q = (xn @ Wq.T + bq).reshape(Bx, Nx, H, D).transpose(0, 2, 1, 3)
        k = (xn @ Wk.T + bk).reshape(Bx, Nx, H, D).transpose(0, 2, 1, 3)
        v = (xn @ Wv.T + bv).reshape(Bx, Nx, H, D).transpose(0, 2, 1, 3)
        attn = jnp.einsum('bhnd,bhmd->bhnm', q, k) * scale
        M = _interp_matrix(Nx, BIAS_S)
        rel = jnp.einsum('ni,hij,mj->hnm', M, rel_bias, M)
        rel = rel.at[:, -1, :].set(0.0).at[:, :, -1].set(0.0)
        attn = attn + rel[None]
        mask = jnp.triu(jnp.ones((Nx, Nx), dtype=bool), k=1)
        attn = jnp.where(mask, -jnp.inf, attn)
        attn = jax.nn.softmax(attn, axis=-1)
        out = jnp.einsum('bhnm,bhmd->bhnd', attn, v)
        out = out.transpose(0, 2, 1, 3).reshape(Bx, Nx, C)
        out = out @ Wo.T + bo
        return out

    def _L3_xattn_ref(query, key, value, wq, wk, wv, bq, bk, bv):
        import jax, jax.numpy as jnp
        import numpy as np
        import math
        IN_C = 128
        OUT_C = 128
        HEADS = 16
        GROUPS = 4

        def grouped_linear(src, weight, bias):
            g, icg, ocg = weight.shape
            lead = src.shape[:-1]
            s = src.reshape(*lead, g, icg)
            out = jnp.einsum('...gi,gio->...go', s, weight)
            out = out.reshape(*lead, g * ocg)
            return out + bias

        def restricted_softmax(src, margin=0.0):
            src_max = jnp.maximum(jnp.max(src, axis=-1, keepdims=True), 0.0)
            out = jnp.exp(src - src_max)
            return out / (jnp.sum(out, axis=-1, keepdims=True) + jnp.exp(margin - src_max))
        q = grouped_linear(query, wq, bq)
        k = grouped_linear(key, wk, bk)
        v = grouped_linear(value, wv, bv)
        B, Sq, _ = q.shape
        Sk = k.shape[-2]
        d = OUT_C // HEADS
        q = q.reshape(B, Sq, HEADS, d).transpose(0, 2, 1, 3)
        k = k.reshape(B, Sk, HEADS, d).transpose(0, 2, 1, 3)
        v = v.reshape(B, Sk, HEADS, d).transpose(0, 2, 1, 3)
        score = jnp.einsum('bhqd,bhkd->bhqk', q, k) / math.sqrt(d)
        attn = restricted_softmax(score)
        out = jnp.einsum('bhqk,bhkd->bhqd', attn, v)
        out = out.transpose(0, 2, 1, 3).reshape(B, Sq, OUT_C)
        return out

    def _L3_ffn_ref(hidden_states, wr, w1, b1, w2, b2):
        import jax, jax.numpy as jnp
        import numpy as np
        TOP_K = 2
        CAP_FACTOR = 1.25

        def _gelu(x):
            return 0.5 * x * (1.0 + jnp.tanh(jnp.sqrt(2.0 / jnp.pi) * (x + 0.044715 * x ** 3)))
        B, S, D = hidden_states.shape
        E = wr.shape[0]
        x = hidden_states.reshape(-1, D)
        T = x.shape[0]
        logits = x @ wr.T
        vals, idx = jax.lax.top_k(logits, TOP_K)
        sparse = jnp.full((T, E), -jnp.inf, dtype=logits.dtype)
        sparse = sparse.at[jnp.arange(T)[:, None], idx].set(vals)
        gating = jax.nn.softmax(sparse, axis=-1)
        cap = max(8, int(max(1, T * TOP_K // E) * CAP_FACTOR))
        mask = (idx[:, :, None] == jnp.arange(E)).any(axis=1)
        pos = jnp.cumsum(mask.astype(jnp.int32), axis=0) - 1
        keep = mask & (pos < cap)
        slot = jnp.where(keep, pos, cap)
        e_grid = jnp.broadcast_to(jnp.arange(E)[None, :], (T, E))
        t_grid = jnp.broadcast_to(jnp.arange(T)[:, None], (T, E))
        dispatch = jnp.full((E, cap + 1), T, dtype=jnp.int32)
        dispatch = dispatch.at[e_grid, slot].set(t_grid)[:, :cap]
        x_pad = jnp.concatenate([x, jnp.zeros((1, D), x.dtype)], axis=0)
        g_pad = jnp.concatenate([gating, jnp.zeros((1, E), gating.dtype)], axis=0)
        xg = x_pad[dispatch]
        h = _gelu(jnp.einsum('ecd,edf->ecf', xg, w1) + b1[:, None, :])
        y = jnp.einsum('ecf,efd->ecd', h, w2) + b2[:, None, :]
        g = g_pad[dispatch, jnp.arange(E)[:, None]]
        wy = y * g[..., None]
        out = jax.ops.segment_sum(wy.reshape(-1, D), dispatch.reshape(-1), num_segments=T + 1)[:T]
        return out.reshape(B, S, D)
    x = x + _L0_attn_ref(_layernorm(x, axis=-1), L0_attn_Wq, L0_attn_Wk, L0_attn_Wv, L0_attn_Wo, L0_attn_lq1, L0_attn_lk1, L0_attn_lq2, L0_attn_lk2, L0_attn_ln_g, L0_attn_ln_b)
    x = x + _L0_xattn_ref(ctx_1024, _layernorm(x, axis=-1))
    x = x + _L0_ffn_ref(_layernorm(x, axis=-1), L0_ffn_q_node_w, L0_ffn_q_node_b, L0_ffn_q_w1, L0_ffn_q_b1, L0_ffn_q_w2, L0_ffn_q_b2, L0_ffn_k_node_w, L0_ffn_k_node_b, L0_ffn_k_w1, L0_ffn_k_b1, L0_ffn_k_w2, L0_ffn_k_b2, L0_ffn_v_node_w, L0_ffn_v_node_b, L0_ffn_v_w1, L0_ffn_v_b1, L0_ffn_v_w2, L0_ffn_v_b2)
    x = x + _L1_attn_ref(_layernorm(x, axis=-1), L1_attn_Wqkv, L1_attn_bqkv, L1_attn_Wout, L1_attn_bout)
    x = x + _L1_xattn_ref(_layernorm(x, axis=-1), ctx_1024, L1_xattn_q_w, L1_xattn_k_w, L1_xattn_norm_w, L1_xattn_gate_w, L1_xattn_gate_b)
    x = x + _L1_ffn_ref(_layernorm(x, axis=-1), L1_ffn_gate_w, L1_ffn_gate_b, L1_ffn_sh_w1, L1_ffn_sh_b1, L1_ffn_sh_w2, L1_ffn_sh_b2, L1_ffn_ew1, L1_ffn_eb1, L1_ffn_ew2, L1_ffn_eb2)
    x = x + _L2_attn_ref(_layernorm(x, axis=-1), L2_attn_attention_mask, L2_attn_Wq, L2_attn_bq, L2_attn_Wqa, L2_attn_bqa, L2_attn_Wk, L2_attn_bk, L2_attn_Wka, L2_attn_bka, L2_attn_Wv, L2_attn_bv, L2_attn_gamma, L2_attn_beta)
    x = x + _L2_xattn_ref(_layernorm(x, axis=-1), ctx_1024, ctx_1024, L2_xattn_wq, L2_xattn_bq, L2_xattn_wk, L2_xattn_bk, L2_xattn_wv, L2_xattn_bv, L2_xattn_wo, L2_xattn_bo)
    x = x + _L2_ffn_ref(_layernorm(x, axis=-1), L2_ffn_W1, L2_ffn_b1, L2_ffn_W2, L2_ffn_b2)
    x = x + _L3_attn_ref(_layernorm(x, axis=-1), L3_attn_Wq, L3_attn_bq, L3_attn_Wk, L3_attn_bk, L3_attn_Wv, L3_attn_bv, L3_attn_Wo, L3_attn_bo, L3_attn_gamma, L3_attn_beta, L3_attn_rel_bias)
    x = x + _L3_xattn_ref(_layernorm(x, axis=-1), ctx_1024, ctx_1024, L3_xattn_wq, L3_xattn_wk, L3_xattn_wv, L3_xattn_bq, L3_xattn_bk, L3_xattn_bv)
    x = x + _L3_ffn_ref(_layernorm(x, axis=-1), L3_ffn_wr, L3_ffn_w1, L3_ffn_b1, L3_ffn_w2, L3_ffn_b2)
    return x

_drawn_inputs = setup_inputs


def setup_inputs(seed=0):
    import zlib

    import numpy as np

    out = dict(_drawn_inputs(seed))
    spreads = {'L0_attn_ln_g': (1.0, 0.2),
     'L0_attn_ln_b': (0.0, 0.1),
     'L0_ffn_q_b1': (0.0, 0.8),
     'L0_ffn_q_b2': (0.0, 0.8),
     'L0_ffn_k_b1': (0.0, 0.8),
     'L0_ffn_k_b2': (0.0, 0.8),
     'L0_ffn_v_b1': (0.0, 0.47),
     'L0_ffn_v_b2': (0.0, 0.325),
     'L1_xattn_norm_w': (1.0, 0.6),
     'L1_xattn_gate_b': (0.0, 0.537),
     'L1_ffn_gate_b': (0.0, 0.1),
     'L1_ffn_sh_b1': (0.0, 0.44),
     'L1_ffn_sh_b2': (0.0, 0.1),
     'L1_ffn_eb1': (0.0, 0.59),
     'L1_ffn_eb2': (0.0, 0.376),
     'L2_attn_bq': (0.0, 2.0),
     'L2_attn_Wqa': (0.0, 2.0),
     'L2_attn_bqa': (1.0, 0.6),
     'L2_attn_bk': (0.0, 2.0),
     'L2_attn_Wka': (0.0, 2.0),
     'L2_attn_bka': (1.0, 0.6),
     'L2_attn_bv': (0.0, 2.0),
     'L2_attn_gamma': (1.0, 0.6),
     'L2_attn_beta': (0.0, 2.0),
     'L3_attn_bq': (0.0, 2.0),
     'L3_attn_bk': (0.0, 2.0),
     'L3_attn_bv': (0.0, 2.0),
     'L3_attn_bo': (0.0, 2.0),
     'L3_attn_gamma': (1.0, 0.6),
     'L3_attn_beta': (0.0, 2.0),
     'L3_ffn_b1': (0.0, 2.0),
     'L3_ffn_b2': (0.0, 2.0)}
    factors = {'L0_attn_lq1': 3.276,
     'L0_ffn_q_node_b': 6.181,
     'L0_ffn_k_node_b': 5.27,
     'L1_attn_bqkv': 2.828,
     'L2_attn_Wq': 64.0,
     'L2_attn_Wk': 64.0,
     'L2_attn_Wv': 64.0,
     'L2_xattn_bq': 8.0,
     'L2_xattn_bk': 200.0,
     'L2_ffn_b1': 8.0,
     'L2_ffn_b2': 200.0,
     'L3_attn_Wq': 8.0,
     'L3_attn_Wk': 8.0,
     'L3_attn_Wv': 8.0,
     'L3_attn_Wo': 8.0,
     'L3_attn_rel_bias': 200.0,
     'L3_xattn_wq': 8.0,
     'L3_xattn_wk': 8.0,
     'L3_xattn_wv': 8.0,
     'L3_xattn_bq': 31.637,
     'L3_xattn_bk': 178.761,
     'L3_xattn_bv': 64.0,
     'L3_ffn_wr': 8.0,
     'L3_ffn_w1': 8.0,
     'L3_ffn_w2': 8.0}
    for name, (base, spread) in spreads.items():
        noise = np.random.default_rng([zlib.crc32(name.encode()), seed]).standard_normal(out[name].shape)
        drawn = base * np.exp(spread * noise) if base else spread * noise
        out[name] = jnp.asarray(drawn.astype(out[name].dtype))
    for name, factor in factors.items():
        out[name] = (out[name] * factor).astype(out[name].dtype)
    return out
```

```python
from contextlib import ExitStack

import concourse.bass as bass
from concourse import mybir

F32 = mybir.dt.float32
BF16 = mybir.dt.bfloat16
ALU = mybir.AluOpType
ACT = mybir.ActivationFunctionType
AX = mybir.AxisListType

P = 128
NB, SL = 64, 64
NT = NB * SL // P
GT = 4
NG = NT // GT
GN = GT * P
NH = 16
HP = NH // 2
NEG = -1.0e30
LN_EPS = 1e-5

MATS = ["a0_q", "a0_k", "a0_v", "a0_o", "a1_q", "a1_k", "a1_v", "a1_o", "x1_q", "x1_k", "x1_g",
        "a2_q", "a2_k", "a2_v", "a2_qa", "a2_ka", "x2_q", "x2_k", "x2_v", "x2_o",
        "a3_q", "a3_k", "a3_v", "a3_o", "x3_q", "x3_k", "x3_v"]
COLS = ["a1_bq", "a1_bk", "x1_nw", "a2_ga", "a2_be", "a2_bq", "x2_bq", "x2_bk",
        "a3_bq", "a3_bk", "a3_ga", "a3_be", "x3_bq", "x3_bk"]
ROWS = ["a0_g", "a0_b", "a1_bv", "a1_bo", "x1_gb", "x1_nw", "a2_bq", "a2_bk", "a2_bv", "a2_bqa", "a2_bka",
        "x2_bv", "x2_bo", "a3_bv", "a3_bo", "x3_bv", "f2_b2"]


class Signal:

    def __init__(self, sem, per):
        self.sem, self.per = sem, per

    def after(self, g, k=None):
        return g * self.per + (self.per if k is None else k)


class Chain:

    def __init__(self, sem, per):
        self.sem, self.per, self.k, self.base = sem, per, 0, 0

    def link(self, eng, ins, g=0):
        ins.then_inc(self.sem, 1)
        self.k += 1
        eng.wait_ge(self.sem, g * self.per + self.base + self.k)

    def loop(self):
        self.base, self.k = self.base + self.k, 0

    def close(self):
        assert self.k == self.per, (self.k, self.per)


class Links:

    def __init__(self, sem):
        self.sem, self.k, self.dyn = sem, 0, 0

    def link(self, eng, ins, g=None):
        ins.then_inc(self.sem, 1)
        self.k += 1
        eng.wait_ge(self.sem, self.dyn + self.k)

    def enter(self, i, per):
        self.dyn, self.per, self.start = i * per, per, self.k

    def leave(self, n):
        assert self.k - self.start == self.per, (self.k - self.start, self.per)
        self.k, self.dyn = self.start + n * self.per, 0


def pipeline(eng, body, links=None, per=0):
    body(0, 0, True, False)
    n = (NG - 2) // 2
    with eng.Fori(0, n) as i:
        if links:
            links.enter(i, 2 * per)
        for u in range(2):
            body(i * 2 + (1 + u), (1 + u) % 2, False, False)
    if links:
        links.leave(n)
    body(NG - 1, (NG - 1) % 2, False, True)


def flat(ap):
    return ap.rearrange("p a b -> p (a b)")


def bc(ap, axis, shape):
    return ap.unsqueeze(axis).to_broadcast(shape)


class Phase:

    def __init__(self, nc, tag):
        self.nc, self.tag, self.ctx, self.sems = nc, tag, ExitStack(), []

    def sb(self, name, shape, dt=F32):
        return self.ctx.enter_context(self.nc.sbuf_tensor(f"{self.tag}_{name}", shape, dt))

    def ps(self, name, shape, dt=F32):
        return self.ctx.enter_context(self.nc.psum_tensor(f"{self.tag}_{name}", shape, dt))

    def counter(self, name, per=1):
        s = self.nc.alloc_semaphore(f"{self.tag}_{name}")
        self.sems.append(s)
        return Signal(s, per)

    def links(self, name):
        s = self.nc.alloc_semaphore(f"{self.tag}_{name}")
        self.sems.append(s)
        return Links(s)

    def chain(self, name, per):
        s = self.nc.alloc_semaphore(f"{self.tag}_{name}")
        self.sems.append(s)
        return Chain(s, per)

    def close(self):
        self.ctx.close()
        self.nc.clear_and_free_semaphores(self.sems)
        self.nc.all_engine_barrier()


class Norm:

    LINKS = 3

    def __init__(self, ph, tag="ln", width=1, out=None):
        self.stats = ph.sb(f"{tag}_stats", [P, GT, 6])
        self.mv = ph.sb(f"{tag}_mv", [P, GT, 2])
        self.var = ph.sb(f"{tag}_var", [P, GT])
        self.rstd = ph.sb(f"{tag}_rstd", [P, GT])
        self.xn = out if out is not None else ph.sb(f"{tag}_xn", [P, GT, P])
        self.var_ready = ph.counter(f"{tag}_var_ready")
        self.rstd_ready = ph.counter(f"{tag}_rstd_ready")
        self.xn_ready = ph.counter(f"{tag}_xn_ready")

    def stats_part(self, v, chain, g, src, eps=LN_EPS):
        for t in range(GT):
            last = v.bn_stats(self.stats[:, t, :], src(t))
        chain.link(v, last, g)
        v.memset(self.var[:, :], 0.0)
        for t in range(GT):
            last = v.bn_aggr(self.mv[:, t, :], self.stats[:, t, :])
        chain.link(v, last, g)
        v.tensor_scalar(self.var[:, :], self.mv[:, :, 1], eps, None, ALU.add).then_inc(self.var_ready.sem, 1)

    def pool_part(self, pool, k, g):
        pool.wait_ge(self.var_ready.sem, self.var_ready.after(g))
        pool.tensor_tensor(self.rstd[:, :], self.var[:, :], k.neghalf[:, 0:GT], ALU.pow).then_inc(self.rstd_ready.sem, 1)

    def scale_part(self, v, chain, g, src):
        v.wait_ge(self.rstd_ready.sem, self.rstd_ready.after(g))
        for t in range(GT):
            last = v.tensor_scalar(self.xn[:, t, :], src(t), self.mv[:, t, 0:1], self.rstd[:, t:t + 1],
                                   ALU.subtract, ALU.mult)
        last.then_inc(self.xn_ready.sem, 1)
        v.wait_ge(self.xn_ready.sem, self.xn_ready.after(g))


class Core:
    pass


def load_experts(eng, k, d, tag, n, sem):
    eng.dma_start(k.moe[:, 0:n * 512], d[f"{tag}_w1"]).then_inc(sem, 16)
    eng.dma_start(k.moe[:, n * 512:2 * n * 512], d[f"{tag}_w2"]).then_inc(sem, 16)


def load_all(nc, k, d):
    ph = Phase(nc, "load")
    loaded = ph.counter("loaded")
    made = ph.counter("made")
    block = nc.Block()
    with block:
        @block.sync
        def _(sp):
            sp.dma_start(k.x[:, :, :], d["x"].rearrange("(t p) d -> p t d", p=P)).then_inc(loaded.sem, 16)
            sp.dma_start(k.cols[:, :], d["cols"]).then_inc(loaded.sem, 16)
            sp.dma_start(k.rows[:, :, :], d["rows"].rearrange("p (r n) -> p r n", n=P)).then_inc(loaded.sem, 16)
            sp.wait_ge(loaded.sem, 48)

        @block.scalar
        def _(act):
            act.dma_start(k.mats[:, :, :], d["mats"].rearrange("p (m n) -> p m n", n=P)).then_inc(made.sem, 16)
            act.dma_start(k.ident[:, :], d["ident"]).then_inc(made.sem, 16)
            act.wait_ge(made.sem, 32)
            act.wait_ge(loaded.sem, 48)
            act.dma_start(k.f0w[:, 0:3072], d["f0_w1"]).then_inc(k.f0_in, 16)
            act.dma_start(k.f0w[:, 3072:6144], d["f0_w2"]).then_inc(k.f0_in, 16)
            load_experts(act, k, d, "f1", 9, k.f1_in)

        @block.gpsimd
        def _(pool):
            pool.memset(k.neghalf[:, :], -0.5)
    ph.close()



def attention(nc, k, d, tag, q, kk, vv, o=None, kv="self", width=8, qb=None, kb=None, vb=None,
              ob=None, affine=None, bias=False, restricted=False, diff=None):
    ph = Phase(nc, tag)
    W1 = width + 1
    norm = Norm(ph)
    norm2 = Norm(ph, "ln2") if affine else None
    normed = norm2 if affine else norm
    cross = kv == "ctx"
    ctxb = ph.sb("ctx", [P, GT, P]) if cross else None
    xT = ph.sb("xT", [P, GT, 192])
    cT = ph.sb("cT", [P, GT, 192]) if cross else xT
    qT = ph.sb("qT", [P, GN])
    qz = ph.sb("qz", [P, 2, 4, GN])
    kT = ph.sb("kT", [P, GN])
    kbd = ph.sb("kbd", [P, 2, 2 * GT, 4, SL])
    mask4 = ph.sb("mask4", [P, 4])
    vx = ph.sb("vx", [P, 2, GT, 2, NH, W1])
    mx = ph.sb("mx", [P, 2, 32])
    em = ph.sb("em", [P, 2, 32]) if restricted else None
    e = ph.sb("e", [P, 2, 32, SL])
    pT = ph.sb("pT", [P, 2, HP, P])
    rs = ph.sb("rs", [P, 2, NH])
    att = ph.sb("att", [P, GT, P])
    attT = ph.sb("attT", [P, GT, P]) if o is not None else None
    S = ph.ps("S", [P, 4, 512])
    TP = ph.ps("TP", [P, 2, 512])
    AV = ph.ps("AV", [P, 512])
    PJ = ph.ps("PJ", [P, 512])

    place = lambda t: TP[:, 0, :] if t % 2 else AV

    setup_in = ph.counter("setup_in")
    setup_done = ph.counter("setup_done")
    ctx_in = ph.counter("ctx_in", 16)
    x_transposed, c_transposed = ph.counter("x_transposed"), ph.counter("c_transposed")
    xT_ready, cT_ready = ph.counter("xT_ready"), ph.counter("cT_ready")
    q_product, k_product = ph.counter("q_product"), ph.counter("k_product")
    q_spread, qz_zeroed = ph.counter("q_spread"), ph.counter("qz_zeroed")
    q_ready, kT_ready, kbd_ready = ph.counter("q_ready"), ph.counter("kT_ready"), ph.counter("kbd_ready")
    vn_product, vs_product = ph.counter("vn_product"), ph.counter("vs_product")
    vn_taken, v_ready = ph.counter("vn_taken"), ph.counter("v_ready")
    scores = ph.counter("scores", 2)
    shifted = ph.counter("shifted", 2)
    em_ready = ph.counter("em_ready", 2)
    weights = ph.counter("weights", 2)
    turned = ph.counter("turned", 8)
    pT_half = ph.counter("pT_half", 8)
    values = ph.counter("values", 4)
    values_taken = ph.counter("values_taken", 4)
    att_ready = ph.counter("att_ready", 2)
    att_turned, attT_ready, projected = ph.counter("att_turned"), ph.counter("attT_ready"), ph.counter("projected")
    x_updated = ph.counter("x_updated")
    af, re, di = bool(affine), restricted, bool(diff)
    per = 2 * (1 + af) + 2 * (1 + re + bool(bias)) + 4 * (1 + re + di) + 16 * di + (ob is not None)
    links = ph.links("dve_links")
    bt_ready = ph.counter("bt_ready")
    setup_chain = ph.chain("dve_setup", 0)

    if diff:
        lam = ph.sb("lam", [P, 8])
        lq = ph.sb("lq", [P, 4, 8])
        lqp = ph.sb("lqp", [P, 2, 8])
        lsum = ph.sb("lsum", [P, 4])
        two = ph.sb("two", [P, NH, width])
        raw = ph.sb("raw", [P, GT * 8, width])
        sq = ph.sb("sq", [P, GT * 8, width])
        hs = ph.sb("hs", [P, 3, GT * 8])
        lam_in, lam_exp = ph.counter("lam_in"), ph.counter("lam_exp")
        hvar_ready, hrstd_ready = ph.counter("hvar_ready", 2), ph.counter("hrstd_ready", 2)
    if bias:
        relT = ph.sb("relT", [32, NH, 32])
        mt = ph.sb("mt", [32, 192])
        u = ph.sb("u", [32, NH, SL])
        causal = ph.sb("causal", [P, SL])
        bt = ph.sb("bt", [P, NH, SL])
        u_product, u_ready, bt_product = ph.counter("u_product"), ph.counter("u_ready"), ph.counter("bt_product")

    block = nc.Block()
    with block:
        @block.sync
        def _(sp):
            sp.dma_start(mask4[:, :], d["mask4"]).then_inc(setup_in.sem, 16)
            if diff:
                sp.dma_start(lq[:, :, :], d["lq"].rearrange("p (a b) -> p a b", b=8)).then_inc(setup_in.sem, 16)
            if bias:
                sp.dma_start(relT[:, :, :], d["relT"].rearrange("p (a b) -> p a b", b=32)).then_inc(setup_in.sem, 16)
                sp.dma_start(mt[:, :], d["interpT"]).then_inc(setup_in.sem, 16)
                sp.dma_start(causal[:, :], d["causal"]).then_inc(setup_in.sem, 16)
            if cross:
                src = d["ctx"].rearrange("(t p) d -> p t d", p=P)
                sp.dma_start(ctxb[:, :, :], src[:, 0:GT, :]).then_inc(ctx_in.sem, 16)
                with sp.Fori(1, NG) as g:
                    sp.wait_ge(c_transposed.sem, c_transposed.after(g - 1))
                    sp.dma_start(ctxb[:, :, :], src[:, bass.ds(g * GT, GT), :]).then_inc(ctx_in.sem, 16)

        n_setup = 16 * (1 + (1 if diff else 0) + (3 if bias else 0))

        @block.gpsimd
        def _(pool):
            for half in range(2):
                last = pool.memset(vx[64 * half:64 * half + 64, :, :, :, :, :].rearrange("p z a b c d -> p (z a b c d)"), 0.0)
            last.then_inc(setup_done.sem, 1)
            pool.wait_ge(setup_done.sem, 1)
            for half in range(2):
                col = vx[64 * half:64 * half + 64, :, :, :, half:NH:2, width].rearrange("p z a b c -> p (z a b) c")
                last = pool.memset(col, 1.0)
            last.then_inc(setup_done.sem, 1)
            pool.wait_ge(setup_in.sem, n_setup)

            def norms(g):
                norm.pool_part(pool, k, g)
                if affine:
                    norm2.pool_part(pool, k, g)

            def keys(g, par):
                pool.wait_ge(kT_ready.sem, kT_ready.after(g))
                shape = [P, 2 * GT, 4, SL]
                pool.tensor_tensor(kbd[:, par, :, :, :],
                                   bc(kT[:, :].rearrange("p (b j) -> p b j", j=SL), 2, shape),
                                   mask4[:, :].unsqueeze(1).unsqueeze(3).to_broadcast(shape),
                                   ALU.mult).then_inc(kbd_ready.sem, 1)

            def head_norms(g, p):
                pool.wait_ge(hvar_ready.sem, hvar_ready.after(g, p + 1))
                n = slice(16 * p, 16 * p + 16)
                pool.tensor_tensor(hs[:, 2, n], hs[:, 1, n], k.neghalf[:, n], ALU.pow).then_inc(hrstd_ready.sem, 1)

            def body(g, par, first, last):
                if not last:
                    norms(g + 1)
                if diff and not first:
                    head_norms(g - 1, 1)
                if not last:
                    keys(g + 1, 1 - par)
                if diff:
                    head_norms(g, 0)

            norms(0)
            keys(0, 0)
            pipeline(pool, body)
            if diff:
                head_norms(NG - 1, 1)

        @block.vector
        def _(v):
            if diff:
                v.wait_ge(setup_in.sem, n_setup)
                setup_chain.link(v, v.tensor_tensor(lqp[:, :, :], lq[:, 0:4:2, :], lq[:, 1:4:2, :], ALU.mult))
                v.tensor_reduce(lsum[:, 0:2], lqp[:, :, :], AX.X, ALU.add).then_inc(lam_in.sem, 1)
                v.wait_ge(lam_exp.sem, 1)
                setup_chain.link(v, v.tensor_tensor(lam[:, 0:1], lsum[:, 3:4], lsum[:, 2:3], ALU.subtract))
                setup_chain.link(v, v.tensor_scalar(lam[:, 1:2], lam[:, 0:1], -diff, None, ALU.add))
            if bias:
                v.wait_ge(bt_product.sem, 1)
                for n in range(2):
                    last = v.tensor_tensor(bt[:, 8 * n:8 * n + 8, :], S[:, 2 + n, :].rearrange("p (h j) -> p h j", j=SL),
                                           bc(causal[:, :], 1, [P, 8, SL]), ALU.add)
                last.then_inc(bt_ready.sem, 1)
            v.memset(qz[:, :, :, :], 0.0).then_inc(qz_zeroed.sem, 1)
            v.wait_ge(qz_zeroed.sem, 1)
            v.wait_ge(setup_done.sem, 2)

            def norm_stats(g):
                norm.stats_part(v, links, g, lambda t: flat(k.x[:, bass.ds(g * GT + t, 1), :]))

            def norm_scale(g):
                norm.scale_part(v, links, g, lambda t: flat(k.x[:, bass.ds(g * GT + t, 1), :]))
                if affine:
                    xn_t = lambda t: norm.xn[:, t, :]
                    norm2.stats_part(v, links, g, xn_t)
                    norm2.scale_part(v, links, g, xn_t)

            def shift(g, p):
                v.wait_ge(scores.sem, scores.after(g, p + 1))
                Sv = S[:, :, :].rearrange("p r (n j) -> p (r n) j", j=SL)
                if bias:
                    for a in range(2):
                        cols = slice(256 * a, 256 * a + 256)
                        last = v.tensor_tensor(e[:, p, :, :].rearrange("p (r a h) j -> p r a (h j)", r=4, a=2)[:, :, a, :],
                                               S[:, :, cols], bt[:, :, :].rearrange("p (r h) j -> p r (h j)", r=4), ALU.add)
                    links.link(v, last)
                    Sv = e[:, p, :, :]
                links.link(v, v.tensor_reduce(mx[:, p, :], Sv, AX.X, ALU.max))
                if restricted:
                    links.link(v, v.tensor_scalar(mx[:, p, :], mx[:, p, :], 0.0, None, ALU.max))
                v.tensor_tensor(e[:, p, :, :], Sv, bc(mx[:, p, :], 2, [P, 32, SL]), ALU.subtract).then_inc(shifted.sem, 1)

            def take_values(g, t):
                v.wait_ge(values.sem, values.after(g, t + 1))
                av = place(t)[:, 0:NH * W1].rearrange("p (h w) -> p h w", w=W1)
                if restricted:
                    v.wait_ge(em_ready.sem, em_ready.after(g, t // 2 + 1))
                    emt = em[:, t // 2, :].rearrange("p (r a h) -> p r a h", a=2, h=4)[:, :, t % 2, :]
                    links.link(v, v.tensor_tensor(rs[:, t % 2, :].rearrange("p (r h) -> p r h", h=4),
                                                  av[:, :, width].rearrange("p (r h) -> p r h", h=4), emt, ALU.add))
                    links.link(v, v.reciprocal(rs[:, t % 2, :], rs[:, t % 2, :]))
                else:
                    links.link(v, v.reciprocal(rs[:, t % 2, :], av[:, :, width]))
                if diff:
                    links.link(v, v.tensor_scalar(rs[:, t % 2, 1:NH:2], rs[:, t % 2, 1:NH:2], lam[:, 1:2], None, ALU.mult))
                    v.tensor_tensor(two[:, :, :], av[:, :, 0:width], bc(rs[:, t % 2, :], 2, [P, NH, width]), ALU.mult)\
                        .then_inc(values_taken.sem, 1)
                    v.wait_ge(values_taken.sem, values_taken.after(g, t + 1))
                    last = v.tensor_tensor(raw[:, 8 * t:8 * t + 8, :], two[:, 0:NH:2, :], two[:, 1:NH:2, :], ALU.add)
                    if t % 2:
                        links.link(v, last)
                else:
                    v.tensor_tensor(att[:, t, :].rearrange("p (h w) -> p h w", w=width),
                                    av[:, :, 0:width], bc(rs[:, t % 2, :], 2, [P, NH, width]), ALU.mult).then_inc(values_taken.sem, 1)

            def spread_q(g, par):
                v.wait_ge(q_ready.sem, q_ready.after(g))
                for r in range(4):
                    rows = slice(32 * r, 32 * r + 32)
                    last = v.tensor_copy(qz[rows, par, r, :], qT[rows, :])
                last.then_inc(q_spread.sem, 1)

            def take_v(g, par, name, prod):
                v.wait_ge(prod.sem, prod.after(g))
                for half in range(2):
                    seq = half if name == "n" else 1 - half
                    rows = slice(64 * half, 64 * half + 64)
                    src = PJ[rows, :].rearrange("p (t h w) -> p t h w", t=GT, w=width)
                    if not diff:
                        src = src[:, :, half:NH:2, :]
                    dst = vx[rows, par, :, seq, half:NH:2, 0:width]
                    if vb is None:
                        last = v.tensor_copy(dst, src)
                    else:
                        bv = k.row(vb)[rows, :].rearrange("p (h w) -> p h w", w=width)[:, half:NH:2, :]
                        last = v.tensor_tensor(dst, src, bc(bv, 1, [64, GT, NH // 2, width]), ALU.add)
                last.then_inc(vn_taken.sem if name == "n" else v_ready.sem, 1)

            def head_stats(g, p):
                n = slice(16 * p, 16 * p + 16)
                shape = [P, 16, width]
                links.link(v, v.tensor_reduce(hs[:, 0, n], raw[:, n, :], AX.X, ALU.add))
                links.link(v, v.tensor_scalar(hs[:, 0, n], hs[:, 0, n], 1.0 / width, None, ALU.mult))
                links.link(v, v.tensor_tensor(raw[:, n, :], raw[:, n, :], bc(hs[:, 0, n], 2, shape), ALU.subtract))
                links.link(v, v.tensor_tensor(sq[:, n, :], raw[:, n, :], raw[:, n, :], ALU.mult))
                links.link(v, v.tensor_reduce(hs[:, 1, n], sq[:, n, :], AX.X, ALU.add))
                v.tensor_scalar(hs[:, 1, n], hs[:, 1, n], 1.0 / width, LN_EPS, ALU.mult, ALU.add).then_inc(hvar_ready.sem, 1)

            def head_scale(g, p):
                n = slice(16 * p, 16 * p + 16)
                v.wait_ge(hrstd_ready.sem, hrstd_ready.after(g, p + 1))
                links.link(v, v.tensor_tensor(raw[:, n, :], raw[:, n, :], bc(hs[:, 2, n], 2, [P, 16, width]), ALU.mult))
                rawt = raw[:, n, :].rearrange("p (t h) w -> p t (h w)", t=2)
                links.link(v, v.tensor_tensor(rawt, rawt, bc(k.row("a0_g"), 1, [P, 2, P]), ALU.mult))
                v.tensor_tensor(att[:, 2 * p:2 * p + 2, :], rawt, bc(k.row("a0_b"), 1, [P, 2, P]), ALU.add).then_inc(att_ready.sem, 1)

            def update(g):
                xg = k.x[:, bass.ds(g * GT, GT), :]
                if o is None:
                    v.wait_ge(values_taken.sem, values_taken.after(g))
                    v.tensor_tensor(xg, xg, att[:, :, :], ALU.add).then_inc(x_updated.sem, 1)
                else:
                    if ob is not None:
                        links.link(v, v.tensor_tensor(xg, xg, bc(k.row(ob), 1, [P, GT, P]), ALU.add))
                    v.wait_ge(projected.sem, projected.after(g))
                    v.tensor_tensor(xg, xg, PJ[:, :].rearrange("p (t d) -> p t d", t=GT), ALU.add).then_inc(x_updated.sem, 1)

            def body(g, par, first, last):
                if not last:
                    norm_stats(g + 1)
                take_v(g, par, "s", vs_product)
                if not last:
                    norm_scale(g + 1)
                shift(g, 0)
                if not first:
                    take_values(g - 1, 2)
                    if diff:
                        head_scale(g - 1, 0)
                    take_values(g - 1, 3)
                    if diff:
                        head_stats(g - 1, 1)
                        head_scale(g - 1, 1)
                shift(g, 1)
                if not first:
                    update(g - 1)
                take_values(g, 0)
                take_values(g, 1)
                if diff:
                    head_stats(g, 0)
                if not last:
                    spread_q(g + 1, 1 - par)
                    take_v(g + 1, 1 - par, "n", vn_product)

            norm_stats(0)
            norm_scale(0)
            spread_q(0, 0)
            take_v(0, 0, "n", vn_product)
            pipeline(v, body, links, per)
            take_values(NG - 1, 2)
            if diff:
                head_scale(NG - 1, 0)
            take_values(NG - 1, 3)
            if diff:
                head_stats(NG - 1, 1)
                head_scale(NG - 1, 1)
            update(NG - 1)

        @block.scalar
        def _(act):
            if diff:
                act.wait_ge(lam_in.sem, 1)
                act.activation(lsum[:, 2:4], lsum[:, 0:2], ACT.Exp).then_inc(lam_exp.sem, 1)
            if bias:
                act.wait_ge(u_product.sem, 1)
                act.copy(u[:, :, :].rearrange("p (a h) j -> p a (h j)", a=2), S[0:32, 0:2, :]).then_inc(u_ready.sem, 1)
            pj = PJ[:, :].rearrange("p (t n) -> p t n", t=GT)

            def project(g, par, first=False):
                act.wait_ge(x_transposed.sem, x_transposed.after(g))
                for lo, hi, n in ((0, 128, 128), (128, 192, 64)):
                    if cross and lo:
                        continue
                    if affine:
                        last = act.activation(xT[:, :, lo:hi], pj[:, :, 0:n], ACT.Identity,
                                              bias=k.col(affine[1]), scale=k.col(affine[0]))
                    else:
                        last = act.copy(xT[:, :, lo:hi], pj[:, :, 0:n])
                last.then_inc(xT_ready.sem, 1)
                if cross:
                    act.wait_ge(c_transposed.sem, c_transposed.after(g))
                    for lo, hi, n in ((0, 128, 128), (128, 192, 64)):
                        last = act.copy(cT[:, :, lo:hi], pj[:, :, 0:n])
                    last.then_inc(cT_ready.sem, 1)
                if not first:
                    act.wait_ge(q_spread.sem, q_spread.after(g - 1))
                for b, prod, dst, done in ((qb, q_product, qT[:, :], q_ready), (kb, k_product, kT[:, :], kT_ready)):
                    act.wait_ge(prod.sem, prod.after(g))
                    if b is None:
                        act.copy(dst, PJ[:, :]).then_inc(done.sem, 1)
                    else:
                        act.activation(dst, PJ[:, :], ACT.Identity, bias=k.col(b)).then_inc(done.sem, 1)

            def turn(g, p):
                for n in range(4):
                    act.wait_ge(turned.sem, turned.after(g, 4 * p + n + 1))
                    act.copy(pT[:, n // 2, 4 * (n % 2):4 * (n % 2) + 4, :],
                             TP[:, n % 2, :].rearrange("p (a b) -> p a b", a=4)).then_inc(pT_half.sem, 1)

            def exps(g, p):
                act.wait_ge(shifted.sem, shifted.after(g, p + 1))
                if restricted:
                    act.activation(em[:, p, :], mx[:, p, :], ACT.Exp, scale=-1.0).then_inc(em_ready.sem, 1)
                act.activation(e[:, p, :, :], e[:, p, :, :], ACT.Exp).then_inc(weights.sem, 1)

            def finish(g):
                if o is not None:
                    act.wait_ge(att_turned.sem, att_turned.after(g))
                    act.copy(attT[:, :, :], pj).then_inc(attT_ready.sem, 1)

            def body(g, par, first, last):
                if not first:
                    turn(g - 1, 1)
                exps(g, 0)
                if not last:
                    project(g + 1, 1 - par)
                if not first:
                    finish(g - 1)
                turn(g, 0)
                exps(g, 1)

            project(0, 0, True)
            pipeline(act, body)
            turn(NG - 1, 1)
            finish(NG - 1)

        @block.tensor
        def _(pe):
            if bias:
                pe.wait_ge(setup_in.sem, n_setup)
                for h in range(NH):
                    last = pe.matmul(S[0:32, h // 8, SL * (h % 8):SL * (h % 8) + SL], relT[:, h, :], mt[:, 128:192],
                                     start=True, stop=True)
                last.then_inc(u_product.sem, 1)
                pe.wait_ge(u_ready.sem, 1)
                for n in range(2):
                    last = pe.matmul(S[:, 2 + n, :], mt[:, 0:128], u[:, 8 * n:8 * n + 8, :], start=True, stop=True)
                last.then_inc(bt_product.sem, 1)
                pe.wait_ge(bt_ready.sem, 1)


            def project(g, first=False):
                pe.wait_ge(normed.xn_ready.sem, normed.xn_ready.after(g))
                if not first:
                    pe.wait_ge(v_ready.sem, v_ready.after(g - 1))
                for t in range(GT):
                    last = pe.transpose(PJ[:, P * t:P * t + P], normed.xn[:, t, :], k.ident[:, :])
                last.then_inc(x_transposed.sem, 1)
                yield
                pe.wait_ge(xT_ready.sem, xT_ready.after(g))
                if cross:
                    pe.wait_ge(ctx_in.sem, ctx_in.after(g))
                    for t in range(GT):
                        last = pe.transpose(PJ[:, P * t:P * t + P], ctxb[:, t, :], k.ident[:, :])
                    last.then_inc(c_transposed.sem, 1)
                    yield
                    pe.wait_ge(cT_ready.sem, cT_ready.after(g))
                pe.matmul(PJ[:, :], k.mat(q), xT[:, :, 0:128], start=True, stop=True).then_inc(q_product.sem, 1)
                yield
                pe.wait_ge(q_ready.sem, q_ready.after(g))
                pe.matmul(PJ[:, :], k.mat(kk), cT[:, :, 0:128], start=True, stop=True).then_inc(k_product.sem, 1)

            def project_v(g, behind=True):
                pe.wait_ge(kT_ready.sem, kT_ready.after(g))
                if behind and o is not None:
                    pe.wait_ge(x_updated.sem, x_updated.after(g - 2))
                for lo, prod in ((0, vn_product), (64, vs_product)):
                    if lo:
                        yield
                        pe.wait_ge(vn_taken.sem, vn_taken.after(g))
                    for t in range(GT):
                        last = pe.matmul(PJ[:, P * t:P * t + P], cT[:, t, lo:lo + 128], k.mat(vv), start=True, stop=True)
                    last.then_inc(prod.sem, 1)

            def score(g, p, par, first=False):
                if p == 0:
                    pe.wait_ge(q_spread.sem, q_spread.after(g))
                    pe.wait_ge(kbd_ready.sem, kbd_ready.after(g))
                if p:
                    pe.wait_ge(shifted.sem, shifted.after(g, 1))
                elif not first:
                    pe.wait_ge(shifted.sem, shifted.after(g - 1))
                for r in range(4):
                    for tt in range(2):
                        for c in range(2):
                            b = 2 * (2 * p + tt) + c
                            last = pe.matmul(S[64 * c:64 * c + 64, r, 256 * tt:256 * tt + 256],
                                             qz[:, par, r, SL * b:SL * b + SL],
                                             kbd[:, par, b, :, :], start=True, stop=True)
                        if r == 3 and tt == 1:
                            last.then_inc(scores.sem, 1)
                        else:
                            yield

            def weigh(g, p, par, very_first=False):
                pe.wait_ge(weights.sem, weights.after(g, p + 1))
                ev = e[:, p, :, :].rearrange("p (r a q h) j -> p r a q (h j)", r=4, a=2, q=2)
                if p:
                    pe.wait_ge(values_taken.sem, values_taken.after(g, 2))
                elif not very_first:
                    pe.wait_ge(values_taken.sem, values_taken.after(g - 1))
                for tt in range(2):
                    for half in range(2):
                        if tt:
                            pe.wait_ge(pT_half.sem, pT_half.after(g, 4 * p + half + 1))
                        for i in range(4):
                            r, q2 = 2 * half + i // 2, i % 2
                            last = pe.transpose(TP[:, half, P * i:P * i + P], ev[:, r, tt, q2, :], k.ident[:, :])
                        last.then_inc(turned.sem, 1)
                if p == 0:
                    pe.wait_ge(v_ready.sem, v_ready.after(g))
                for tt in range(2):
                    t = 2 * p + tt
                    pe.wait_ge(pT_half.sem, pT_half.after(g, 2 * t + 2))
                    for c in range(2):
                        for hp in range(HP):
                            last = pe.matmul(place(t)[64 * c:64 * c + 64, 2 * hp * W1:2 * (hp + 1) * W1],
                                             pT[:, tt, hp, 64 * c:64 * c + 64],
                                             vx[:, par, t, c, 2 * hp:2 * hp + 2, :], start=True, stop=True)
                    last.then_inc(values.sem, 1)

            def finish(g, free):
                if o is None:
                    return
                pe.wait_ge(*free)
                if diff:
                    pe.wait_ge(att_ready.sem, att_ready.after(g))
                else:
                    pe.wait_ge(values_taken.sem, values_taken.after(g))
                for t in range(GT):
                    last = pe.transpose(PJ[:, P * t:P * t + P], att[:, t, :], k.ident[:, :])
                last.then_inc(att_turned.sem, 1)
                yield
                pe.wait_ge(attT_ready.sem, attT_ready.after(g))
                for t in range(GT):
                    last = pe.matmul(PJ[:, P * t:P * t + P], attT[:, t, :], k.mat(o), start=True, stop=True)
                last.then_inc(projected.sem, 1)
                yield

            def mix(between, ahead, *steps):
                for _ in range(ahead):
                    next(between, None)
                for s in steps:
                    for _ in s:
                        next(between, None)
                for _ in between:
                    pass

            def body(g, par, first, last):
                if not first:
                    weigh(g - 1, 1, 1 - par)
                free = (v_ready.sem, v_ready.after(g)) if last else (kT_ready.sem, kT_ready.after(g + 1))
                steps = ([] if last else [project(g + 1)]) + ([] if first else [finish(g - 1, free)])
                mix(score(g, 1, par), 5 if cross else 6, *steps)
                weigh(g, 0, par, first)
                if not last:
                    mix(score(g + 1, 0, 1 - par), 0, project_v(g + 1, not first))

            for _ in project(0, True):
                pass
            mix(score(0, 0, 0, True), 0, project_v(0, False))
            pipeline(pe, body)
            weigh(NG - 1, 1, (NG - 1) % 2)
            for _ in finish(NG - 1, (x_updated.sem, x_updated.after(NG - 2))):
                pass
    ph.close()



def warping(nc, k, d, tag):
    ph = Phase(nc, tag)
    dist_dram = nc.dram_tensor("dist_dram", (NB, SL, SL), F32, kind="Internal").ap()
    path_dram = nc.dram_tensor("path_dram", (NB, SL, SL), F32, kind="Internal").ap()
    SP1 = SL + 1
    BIG = 1.0e30

    with ExitStack() as part:
        outer, ph.ctx = ph.ctx, part
        norm = Norm(ph)
        ctxb, sq, ones = ph.sb("ctx", [P, GT, P]), ph.sb("sq", [P, GT, P]), ph.sb("ones", [P, P])
        xT, xsqT, cT = ph.sb("xT", [P, GN]), ph.sb("xsqT", [P, GN]), ph.sb("cT", [P, GN])
        aa, dist = ph.sb("aa", [P, GT]), ph.sb("dist", [P, GT, SL])
        TX, TC, D2 = ph.ps("TX", [P, 512]), ph.ps("TC", [P, 512]), ph.ps("D2", [P, GT, SL])
        ones_made, ctx_in = ph.counter("ones_made"), ph.counter("ctx_in")
        x_transposed, c_transposed = ph.counter("x_transposed"), ph.counter("c_transposed")
        xT_ready, cT_ready, product = ph.counter("xT_ready"), ph.counter("cT_ready"), ph.counter("product")
        ctx_squared, squares_ready, roots = ph.counter("ctx_squared"), ph.counter("squares_ready"), ph.counter("roots")
        written = ph.counter("written")
        ctx_in.per, written.per = 16, 32
        chain = ph.chain("dve_chain", 3)
        with nc.Block() as block:
            @block.sync
            def _(sp):
                src = d["ctx"].rearrange("(t p) d -> p t d", p=P)
                dst = dist_dram.rearrange("(t c) i j -> c i t j", c=2)
                with sp.Fori(0, NG) as g:
                    sp.wait_ge(c_transposed.sem, g + 1)
                    sp.wait_ge(ctx_squared.sem, g + 1)
                    sp.dma_start(ctxb[:, :, :], src[:, bass.ds(g * GT, GT), :]).then_inc(ctx_in.sem, 16)
                    sp.wait_ge(roots.sem, roots.after(g))
                    for c in range(2):
                        sp.dma_start(dst[c, :, bass.ds(g * GT, GT), :], dist[64 * c:64 * c + 64, :, :]).then_inc(written.sem, 16)
                sp.wait_ge(written.sem, 32 * (NG + 1))

            @block.gpsimd
            def _(pool):
                pool.memset(ones[:, :], 1.0).then_inc(ones_made.sem, 1)
                with pool.Fori(0, NG) as g:
                    norm.pool_part(pool, k, g)

            @block.vector
            def _(v):
                v.memset(aa[:, :], 0.0).then_inc(ctx_squared.sem, 1)
                v.memset(dist[:, :, :], 0.0).then_inc(written.sem, 32)
                with v.Fori(0, NG) as g:
                    x_t = lambda t: flat(k.x[:, bass.ds(g * GT + t, 1), :])
                    norm.stats_part(v, chain, g, x_t)
                    norm.scale_part(v, chain, g, x_t)
                    v.wait_ge(ctx_in.sem, ctx_in.after(g))
                    chain.link(v, v.tensor_tensor(sq[:, :, :], ctxb[:, :, :], ctxb[:, :, :], ALU.mult), g)
                    v.tensor_reduce(aa[:, :], sq[:, :, :], AX.X, ALU.add).then_inc(ctx_squared.sem, 1)
                    v.wait_ge(ctx_squared.sem, ctx_squared.after(g) + 1)
                    v.wait_ge(product.sem, product.after(g))
                    v.wait_ge(written.sem, written.after(g))
                    for t in range(GT):
                        last = v.tensor_scalar(dist[:, t, :], D2[:, t, :], aa[:, t:t + 1], 0.0, ALU.add, ALU.max)
                    last.then_inc(squares_ready.sem, 1)
                chain.close()

            @block.scalar
            def _(act):
                with act.Fori(0, NG) as g:
                    act.wait_ge(x_transposed.sem, x_transposed.after(g))
                    act.copy(xT[:, :], TX[:, :])
                    act.activation(xsqT[:, :], TX[:, :], ACT.Square).then_inc(xT_ready.sem, 1)
                    act.wait_ge(c_transposed.sem, c_transposed.after(g) + 1)
                    act.mul(cT[:, :], TC[:, :], -2.0).then_inc(cT_ready.sem, 1)
                    act.wait_ge(squares_ready.sem, squares_ready.after(g))
                    act.activation(dist[:, :, :], dist[:, :, :], ACT.Sqrt).then_inc(roots.sem, 1)

            @block.tensor
            def _(pe):
                pe.transpose(TC[:, 0:P], k.ident[:, :], k.ident[:, :]).then_inc(c_transposed.sem, 1)
                pe.wait_ge(c_transposed.sem, 1)
                pe.wait_ge(ones_made.sem, 1)
                with pe.Fori(0, NG) as g:
                    pe.wait_ge(norm.xn_ready.sem, norm.xn_ready.after(g))
                    for t in range(GT):
                        last = pe.transpose(TX[:, P * t:P * t + P], norm.xn[:, t, :], k.ident[:, :])
                    last.then_inc(x_transposed.sem, 1)
                    pe.wait_ge(ctx_in.sem, ctx_in.after(g))
                    for t in range(GT):
                        last = pe.transpose(TC[:, P * t:P * t + P], ctxb[:, t, :], k.ident[:, :])
                    last.then_inc(c_transposed.sem, 1)
                    pe.wait_ge(xT_ready.sem, xT_ready.after(g))
                    pe.wait_ge(cT_ready.sem, cT_ready.after(g))
                    for t in range(GT):
                        for c in range(2):
                            tok = slice(P * t + 64 * c, P * t + 64 * c + 64)
                            out = D2[64 * c:64 * c + 64, t, :]
                            pe.matmul(out, cT[:, tok], xT[:, tok], start=True, stop=False)
                            last = pe.matmul(out, ones[:, 0:64], xsqT[:, tok], start=False, stop=True)
                    last.then_inc(product.sem, 1)
        ph.ctx = outer
    nc.clear_and_free_semaphores(ph.sems)
    nc.all_engine_barrier()
    ph.sems = []

    with ExitStack() as part:
        outer, ph.ctx = ph.ctx, part
        D = ph.sb("D", [NB, SL, SL])
        R = ph.sb("R", [NB, SP1, SP1])
        m = ph.sb("m", [NB, SL])
        DU = ph.sb("DU", [NB, SL, 2, SL], BF16)
        L = ph.sb("L", [NB, SL, SP1], BF16)
        AB = ph.sb("AB", [NB, 2, SP1])
        path = ph.sb("path", [NB, SL, SL])
        d_in, path_out = ph.counter("d_in"), ph.counter("path_out")
        path_ready = ph.counter("path_ready")
        fw, bw, st = ph.chain("forward", 2), ph.chain("backward", 3), ph.chain("steps", 0)
        with nc.Block() as block:
            @block.sync
            def _(sp):
                sp.dma_start(D[:, :, :], dist_dram).then_inc(d_in.sem, 16)
                sp.wait_ge(path_ready.sem, 1)
                sp.dma_start(path_dram, D[:, :, :]).then_inc(path_out.sem, 16)
                sp.wait_ge(path_out.sem, 16)

            @block.vector
            def _(v):
                v.memset(flat(R[:, :, :]), BIG)
                v.memset(flat(L[:, :, :]), 0.0)
                st.link(v, v.memset(flat(AB[:, :, :]), 0.0))
                st.link(v, v.memset(R[:, 0, 0:1], 0.0))
                v.wait_ge(d_in.sem, 16)
                with v.Fori(0, SL) as i:
                    row = flat(R[:, bass.ds(i, 1), :])
                    fw.link(v, v.tensor_tensor(m[:, :], row[:, 1:SP1], row[:, 0:SL], ALU.min), i)
                    fw.link(v, v.tensor_tensor_scan(flat(R[:, bass.ds(i + 1, 1), :])[:, 1:SP1], m[:, :],
                                                    flat(D[:, bass.ds(i, 1), :]), BIG, ALU.min, ALU.add), i)
                fw.close()
                cd, cu, cl = R[:, 0:SL, 0:SL], R[:, 0:SL, 1:SP1], R[:, 1:SP1, 0:SL]
                st.link(v, v.tensor_tensor(D[:, :, :], cu, cl, ALU.min))
                v.tensor_tensor(L[:, :, 1:SP1], cu[:, :, ::-1], cl[:, :, ::-1], ALU.is_le)
                st.link(v, v.tensor_tensor(DU[:, :, 0, :], cd[:, :, ::-1], D[:, :, ::-1], ALU.is_le))
                st.link(v, v.tensor_tensor(DU[:, :, 1, :], L[:, :, 1:SP1], DU[:, :, 0, :], ALU.is_gt))
                st.link(v, v.tensor_tensor(D[:, :, :], DU[:, :, 0, :], DU[:, :, 1, :], ALU.add))
                v.tensor_scalar(L[:, :, 1:SP1], D[:, :, :], -1.0, 1.0, ALU.mult, ALU.add)
                st.link(v, v.memset(AB[:, 0, 0:1], 1.0))
                with v.Fori(0, SL) as i:
                    r = SL - 1 - i
                    bw.link(v, v.tensor_tensor(m[:, :], AB[:, 0, 0:SL], AB[:, 1, 1:SP1], ALU.add), i)
                    v.memset(AB[:, 0, 0:1], 0.0)
                    prow = flat(path[:, bass.ds(r, 1), :])
                    bw.link(v, v.tensor_tensor_scan(prow, flat(L[:, bass.ds(r, 1), :])[:, 0:SL],
                                                    m[:, :], 0.0, ALU.mult, ALU.max), i)
                    du = DU[:, bass.ds(r, 1), :, :].rearrange("p a b c -> p (a b) c")
                    bw.link(v, v.tensor_tensor(AB[:, :, 1:SP1], bc(prow, 1, [NB, 2, SL]), du, ALU.mult), i)
                bw.close()
                v.tensor_copy(D[:, :, :], path[:, :, ::-1]).then_inc(path_ready.sem, 1)
        ph.ctx = outer
    nc.clear_and_free_semaphores(ph.sems)
    nc.all_engine_barrier()
    ph.sems = []

    ctxb, pathb = ph.sb("ctx2", [P, 2, GT, P]), ph.sb("pathb", [P, 2, GT, P])
    OUT = ph.ps("OUT", [P, 2, 512])
    cleared = ph.counter("cleared")
    loaded = [ph.counter(f"loaded{u}", 48) for u in range(2)]
    aligned, added = ph.counter("aligned"), ph.counter("added")
    with nc.Block() as block:
        @block.sync
        def _(sp):
            csrc = d["ctx"].rearrange("(t p) d -> p t d", p=P)
            psrc = path_dram.rearrange("(t c) i j -> c i t j", c=2)
            sp.wait_ge(cleared.sem, 1)
            with sp.Fori(0, NG // 2) as i:
                for u in range(2):
                    g = i * 2 + u
                    sp.wait_ge(added.sem, g + 1)
                    sp.dma_start(ctxb[:, u, :, :], csrc[:, bass.ds(g * GT, GT), :]).then_inc(loaded[u].sem, 16)
                    for c in range(2):
                        sp.dma_start(pathb[64 * c:64 * c + 64, u, :, 64 * c:64 * c + 64],
                                     psrc[c, :, bass.ds(g * GT, GT), :]).then_inc(loaded[u].sem, 16)

        @block.gpsimd
        def _(pool):
            pool.memset(pathb[:, :, :, :].rearrange("p a b c -> p (a b c)"), 0.0).then_inc(cleared.sem, 1)

        @block.tensor
        def _(pe):
            with pe.Fori(0, NG // 2) as i:
                for u in range(2):
                    g = i * 2 + u
                    pe.wait_ge(loaded[u].sem, loaded[u].after(i))
                    for t in range(GT):
                        last = pe.matmul(OUT[:, u, P * t:P * t + P], pathb[:, u, t, :], ctxb[:, u, t, :], start=True, stop=True)
                    last.then_inc(aligned.sem, 1)

        @block.vector
        def _(v):
            v.memset(OUT[:, 0, 0:1], 0.0).then_inc(added.sem, 2)
            with v.Fori(0, NG // 2) as i:
                for u in range(2):
                    g = i * 2 + u
                    v.wait_ge(aligned.sem, aligned.after(g))
                    xg = k.x[:, bass.ds(g * GT, GT), :]
                    v.tensor_tensor(xg, xg, OUT[:, u, :].rearrange("p (t n) -> p t n", t=GT), ALU.add).then_inc(added.sem, 1)
    ph.close()



def trees(nc, k, d, tag):
    ph = Phase(nc, tag)
    NC = 8
    norm = Norm(ph)
    nodes, nodeb = ph.sb("nodes", [P, 45]), ph.sb("nodeb", [P, 3, 15])
    b1, b2 = ph.sb("b1", [P, 3 * NC]), ph.sb("b2", [96, 3, P])
    leaf = ph.sb("leaf", [96, 3 * NC, P], mybir.dt.uint16)
    sc = ph.sb("sc", [P, GT * 3, 15])
    gy, gn = ph.sb("gy", [P, GT * 3, 15]), ph.sb("gn", [P, GT * 3, 15])
    s1, s2, s3 = ph.sb("s1", [P, GT * 3, 2]), ph.sb("s2", [P, GT * 3, 4]), ph.sb("s3", [P, GT * 3, 8])
    sel = ph.sb("sel", [P, GT * 3, 32])
    selT, selneg = ph.sb("selT", [96, GN]), ph.sb("selneg", [96, GN], BF16)
    xT = ph.sb("xT", [P, GN])
    xTn, selTn = ph.sb("xTn", [P, GN]), ph.sb("selTn", [96, GN])
    h = ph.sb("h", [P, 4, GN])
    qkvT = ph.sb("qkvT", [P, 3, GN])
    vtok = ph.sb("vtok", [P, GT, P])
    e, mx, rs = ph.sb("e", [P, GT, SL]), ph.sb("mx", [P, GT]), ph.sb("rs", [P, GT])
    ebd = ph.sb("ebd", [P, GT, P])
    eT = ph.sb("eT", [P, GT, P])
    PJ, H, Y, SC = ph.ps("PJ", [P, 512]), ph.ps("H", [P, 4, 512]), ph.ps("Y", [P, 2, 512]), ph.ps("SC", [P, 512])
    setup_in, cleared = ph.counter("setup_in"), ph.counter("cleared")
    x_transposed, xTn_ready, xT_ready = ph.counter("x_transposed"), ph.counter("xTn_ready"), ph.counter("xT_ready")
    selTn_ready = ph.counter("selTn_ready")
    node_scores, sel_ready, sel_turned = ph.counter("node_scores"), ph.counter("sel_ready"), ph.counter("sel_turned")
    selT_ready, hidden = ph.counter("selT_ready", 2), ph.counter("hidden", 3 * NC)
    h_even, h_odd = ph.counter("h_even", 3 * NC // 2), ph.counter("h_odd", 3 * NC // 2)
    tree_out, tree_taken = ph.counter("tree_out", 3), ph.counter("tree_taken", 3)
    v_turned, v_ready, scores = ph.counter("v_turned"), ph.counter("v_ready"), ph.counter("scores")
    shifted, weights, w_turned, wT_ready = ph.counter("shifted"), ph.counter("weights"), ph.counter("w_turned"), ph.counter("wT_ready")
    values, x_updated = ph.counter("values"), ph.counter("x_updated")
    chain = ph.links("dve_chain")
    SCALE = float(P) ** -0.5
    with nc.Block() as block:
        @block.sync
        def _(sp):
            for dst, name in ((nodes[:, :], "f0_nodes"), (flat(nodeb[:, :, :]), "f0_nodeb"), (b1[:, :], "f0_b1"),
                              (flat(b2[:, :, :]), "f0_b2"), (flat(leaf[:, :, :]), "leaf")):
                sp.dma_start(dst, d[name]).then_inc(setup_in.sem, 16)

        @block.gpsimd
        def _(pool):
            pool.memset(flat(ebd[:, :, :]), 0.0)
            pool.memset(flat(sel[:, :, :]), 0.0).then_inc(cleared.sem, 1)
            with pool.Fori(0, NG) as g:
                norm.pool_part(pool, k, g)

        @block.vector
        def _(v):
            v.wait_ge(setup_in.sem, 80)
            v.wait_ge(cleared.sem, 1)

            def stats(g):
                norm.stats_part(v, chain, g, lambda t: flat(k.x[:, bass.ds(g * GT + t, 1), :]))

            def scale(g):
                norm.scale_part(v, chain, g, lambda t: flat(k.x[:, bass.ds(g * GT + t, 1), :]))

            def decide(g):
                v.wait_ge(node_scores.sem, node_scores.after(g))
                chain.link(v, v.tensor_tensor(sc[:, :, :].rearrange("p (t r) n -> p t (r n)", r=3),
                                              SC[:, 0:GT * 45].rearrange("p (t n) -> p t n", t=GT),
                                              bc(flat(nodeb[:, :, :]), 1, [P, GT, 45]), ALU.add))
                v.tensor_scalar(gy[:, :, :], sc[:, :, :], 0.0, None, ALU.is_ge)
                chain.link(v, v.tensor_scalar(gn[:, :, :], sc[:, :, :], 0.0, None, ALU.is_lt))

            def split(n, src, dst):
                w = 2 << n
                v.tensor_tensor(dst[:, :, 0:2 * w:2], src[:, :, :], gn[:, :, w - 1:2 * w - 1], ALU.mult)
                return v.tensor_tensor(dst[:, :, 1:2 * w:2], src[:, :, :], gy[:, :, w - 1:2 * w - 1], ALU.mult)

            def upper_levels(g):
                v.tensor_copy(s1[:, :, 0:1], gn[:, :, 0:1])
                chain.link(v, v.tensor_copy(s1[:, :, 1:2], gy[:, :, 0:1]))
                chain.link(v, split(0, s1, s2[:, :, :]))

            def lower_levels(g):
                chain.link(v, split(1, s2, s3[:, :, :]))
                split(2, s3, sel[:, :, 0:16]).then_inc(sel_ready.sem, 1)

            def keep_leaves(g):
                v.wait_ge(sel_turned.sem, sel_turned.after(g))
                v.tensor_copy(selTn[:, :], SC[0:96, :]).then_inc(selTn_ready.sem, 1)

            def take_leaves(g):
                v.wait_ge(selTn_ready.sem, selTn_ready.after(g))
                v.tensor_copy(selT[:, :], selTn[:, :]).then_inc(selT_ready.sem, 1)
                v.tensor_scalar(selneg[:, :], selTn[:, :], 1.0, -NEG, ALU.subtract, ALU.mult).then_inc(selT_ready.sem, 1)

            routing = {1: stats, 3: scale, 11: decide, 13: upper_levels, 15: lower_levels, 19: keep_leaves}

            def body(g, last_group):
                for n in range(1, 3 * NC, 2):
                    v.wait_ge(hidden.sem, hidden.after(g, n + 1))
                    v.tensor_scalar(h[:, n % 4, :], H[:, n % 4, :], b1[:, n:n + 1], 0.0, ALU.add, ALU.max)\
                        .then_inc(h_odd.sem, 1)
                    if n in routing and not last_group:
                        routing[n](g + 1)
                v.wait_ge(scores.sem, scores.after(g))
                sv = SC[:, 0:GT * SL].rearrange("p (t j) -> p t j", j=SL)
                chain.link(v, v.tensor_reduce(mx[:, :], sv, AX.X, ALU.max))
                v.tensor_tensor(e[:, :, :], sv, bc(mx[:, :], 2, [P, GT, SL]), ALU.subtract).then_inc(shifted.sem, 1)
                if not last_group:
                    take_leaves(g + 1)
                v.wait_ge(weights.sem, weights.after(g))
                chain.link(v, v.tensor_reduce(rs[:, :], ebd[:, :, :], AX.X, ALU.add))
                chain.link(v, v.reciprocal(rs[:, :], rs[:, :]))
                v.wait_ge(values.sem, values.after(g))
                for t in range(GT):
                    xt = flat(k.x[:, bass.ds(g * GT + t, 1), :])
                    last = v.scalar_tensor_tensor(xt, PJ[:, P * t:P * t + P], rs[:, t:t + 1], xt, ALU.mult, ALU.add)
                last.then_inc(x_updated.sem, 1)
                v.wait_ge(x_updated.sem, x_updated.after(g))

            for step in routing.values():
                step(0)
            take_leaves(0)
            with v.Fori(0, NG - 1) as g:
                chain.enter(g, 10)
                body(g, False)
            chain.leave(NG - 1)
            body(NG - 1, True)

        @block.scalar
        def _(act):
            act.wait_ge(setup_in.sem, 80)
            act.wait_ge(cleared.sem, 1)

            def keep_x(g):
                act.wait_ge(x_transposed.sem, x_transposed.after(g))
                act.copy(xTn[:, :], PJ[:, :]).then_inc(xTn_ready.sem, 1)

            def take_x(g):
                act.wait_ge(xTn_ready.sem, xTn_ready.after(g))
                act.copy(xT[:, :], xTn[:, :]).then_inc(xT_ready.sem, 1)

            def body(g, last_group):
                for r in range(3):
                    for c in range(NC):
                        n = r * NC + c
                        if c % 2 == 0:
                            act.wait_ge(hidden.sem, hidden.after(g, n + 1))
                            act.activation(h[:, n % 4, :], H[:, n % 4, :], ACT.Relu, bias=b1[:, n:n + 1]).then_inc(h_even.sem, 1)
                        if n == 8 and not last_group:
                            keep_x(g + 1)
                    act.wait_ge(tree_out.sem, tree_out.after(g, r + 1))
                    act.mul(qkvT[:, r, :], Y[:, r % 2, :], SCALE if r == 0 else 1.0).then_inc(tree_taken.sem, 1)
                if not last_group:
                    take_x(g + 1)
                act.wait_ge(v_turned.sem, v_turned.after(g))
                act.copy(vtok[:, :, :], PJ[:, :].rearrange("p (t n) -> p t n", t=GT)).then_inc(v_ready.sem, 1)
                act.wait_ge(shifted.sem, shifted.after(g))
                for c in range(2):
                    rows = slice(64 * c, 64 * c + 64)
                    last = act.activation(ebd[rows, :, rows], e[rows, :, :], ACT.Exp)
                last.then_inc(weights.sem, 1)
                act.wait_ge(w_turned.sem, w_turned.after(g))
                act.copy(eT[:, :, :], Y[:, 1, :].rearrange("p (t n) -> p t n", t=GT)).then_inc(wT_ready.sem, 1)

            keep_x(0)
            take_x(0)
            with act.Fori(0, NG - 1) as g:
                body(g, False)
            body(NG - 1, True)

        @block.tensor
        def _(pe):
            pe.wait_ge(setup_in.sem, 80)
            pe.wait_ge(k.f0_in, 32)
            w1 = k.f0w[:, 0:3 * 1024].rearrange("p (r n) -> p r n", r=3)
            w2 = k.f0w[:, 3 * 1024:6 * 1024].rearrange("p (r c n) -> p r c n", r=3, c=NC)

            def turn_x(g):
                pe.wait_ge(norm.xn_ready.sem, norm.xn_ready.after(g))
                for t in range(GT):
                    last = pe.transpose(PJ[:, P * t:P * t + P], norm.xn[:, t, :], k.ident[:, :])
                last.then_inc(x_transposed.sem, 1)

            def score_nodes(g):
                pe.wait_ge(xTn_ready.sem, xTn_ready.after(g))
                for t in range(GT):
                    last = pe.matmul(SC[:, 45 * t:45 * t + 45], xTn[:, P * t:P * t + P], nodes[:, :], start=True, stop=True)
                last.then_inc(node_scores.sem, 1)

            def turn_leaves(g):
                pe.wait_ge(sel_ready.sem, sel_ready.after(g))
                for t in range(GT):
                    last = pe.transpose(SC[0:96, P * t:P * t + P], flat(sel[:, 3 * t:3 * t + 3, :]), k.ident[:, :])
                last.then_inc(sel_turned.sem, 1)

            routing = {6: turn_x, 11: score_nodes, 18: turn_leaves}

            def body(g, last_group):
                pe.wait_ge(xT_ready.sem, xT_ready.after(g))
                pe.wait_ge(selT_ready.sem, selT_ready.after(g))

                def make_hidden(n):
                    r, c = n // NC, n % NC
                    pe.matmul(H[:, n % 4, :], w1[:, r, P * c:P * c + P], xT[:, :], start=True, stop=False)
                    pe.matmul(H[:, n % 4, :], leaf[:, n, :].bitcast(BF16), selneg[:, :], start=False, stop=True).then_inc(hidden.sem, 1)

                make_hidden(0)
                make_hidden(1)
                for n in range(3 * NC):
                    r, c = n // NC, n % NC
                    if n + 2 < 3 * NC:
                        make_hidden(n + 2)
                    if n in routing and not last_group:
                        routing[n](g + 1)
                    if c == 0:
                        if r == 2:
                            pe.wait_ge(tree_taken.sem, tree_taken.after(g, 1))
                        pe.matmul(Y[:, r % 2, :], b2[:, r, :], selT[:, :], start=True, stop=False)
                    if c % 2:
                        pe.wait_ge(h_odd.sem, h_odd.after(g, n // 2 + 1))
                    else:
                        pe.wait_ge(h_even.sem, h_even.after(g, n // 2 + 1))
                    last = pe.matmul(Y[:, r % 2, :], w2[:, r, c, :], h[:, n % 4, :], start=False, stop=c == NC - 1)
                    if c == NC - 1:
                        last.then_inc(tree_out.sem, 1)
                pe.wait_ge(tree_taken.sem, tree_taken.after(g, 3))
                if last_group:
                    pe.wait_ge(x_updated.sem, x_updated.after(g - 1))
                else:
                    pe.wait_ge(selTn_ready.sem, selTn_ready.after(g + 1))
                for t in range(GT):
                    last = pe.transpose(PJ[:, P * t:P * t + P], qkvT[:, 2, P * t:P * t + P], k.ident[:, :])
                last.then_inc(v_turned.sem, 1)
                for b in range(2 * GT):
                    c, t = b % 2, b // 2
                    tok = slice(SL * b, SL * b + SL)
                    last = pe.matmul(SC[64 * c:64 * c + 64, SL * t:SL * t + SL], qkvT[:, 0, tok], qkvT[:, 1, tok],
                                     start=True, stop=True)
                last.then_inc(scores.sem, 1)
                pe.wait_ge(weights.sem, weights.after(g))
                for t in range(GT):
                    last = pe.transpose(Y[:, 1, P * t:P * t + P], ebd[:, t, :], k.ident[:, :])
                last.then_inc(w_turned.sem, 1)
                pe.wait_ge(v_ready.sem, v_ready.after(g))
                pe.wait_ge(wT_ready.sem, wT_ready.after(g))
                for t in range(GT):
                    last = pe.matmul(PJ[:, P * t:P * t + P], eT[:, t, :], vtok[:, t, :], start=True, stop=True)
                last.then_inc(values.sem, 1)

            for step in routing.values():
                step(0)
            with pe.Fori(0, NG - 1) as g:
                body(g, False)
            body(NG - 1, True)
    ph.close()



def memory_attention(nc, k, d, tag):
    ph = Phase(nc, tag)
    norm = Norm(ph)
    xn = norm.xn
    sq, ms, r2 = ph.sb("sq", [P, GT, P]), ph.sb("ms", [P, GT]), ph.sb("r2", [P, GT])
    nv = ph.sb("nv", [P, GT, P + 1])
    cv = ph.sb("cv", [P, GT, P + 1])
    mask = ph.sb("mask", [P, 2, SL])
    nT, xT, cT = ph.sb("nT", [P, GN]), ph.sb("xT", [P, GN]), ph.sb("cT", [P, GN])
    qT, kl, km = ph.sb("qT", [P, GN]), ph.sb("kl", [P, GN]), ph.sb("km", [P, GN])
    z, al = ph.sb("z", [P, GT, P]), ph.sb("al", [P, GT, P])
    e, mx, rs = ph.sb("e", [P, GT, 2, SL]), ph.sb("mx", [P, GT]), ph.sb("rs", [P, GT])
    ebd = ph.sb("ebd", [P, GT, 2, P])
    eT = ph.sb("eT", [P, GT, 2, P])
    hh = ph.sb("hh", [P, GT, P])
    PJ, TP, AV, S = ph.ps("PJ", [P, 3, 512]), ph.ps("TP", [P, 2, 512]), ph.ps("AV", [P, 2, 512]), ph.ps("S", [P, GT, 2, SL])
    setup_in, cleared = ph.counter("setup_in"), ph.counter("cleared")
    ctx_in = ph.counter("ctx_in", 16)
    ms_ready, r2_ready, n_ready = ph.counter("ms_ready"), ph.counter("r2_ready"), ph.counter("n_ready")
    turned, turned_taken = ph.counter("turned", 3), ph.counter("turned_taken", 3)
    products, products_taken, gate = ph.counter("products", 3), ph.counter("products_taken", 3), ph.counter("gate")
    z_ready, alpha = ph.counter("z_ready"), ph.counter("alpha")
    scores, shifted, weights = ph.counter("scores"), ph.counter("shifted"), ph.counter("weights")
    w_turned, wT_ready, values = ph.counter("w_turned", 2), ph.counter("wT_ready", 2), ph.counter("values")
    x_updated = ph.counter("x_updated")
    chain = ph.chain("dve_chain", 10)
    with nc.Block() as block:
        @block.sync
        def _(sp):
            sp.dma_start(flat(mask[:, :, :]), d["mask2"]).then_inc(setup_in.sem, 16)
            src = d["ctx"].rearrange("(t p) d -> p t d", p=P)
            sp.wait_ge(cleared.sem, 1)
            with sp.Fori(0, NG) as g:
                sp.wait_ge(x_updated.sem, x_updated.after(g))
                sp.dma_start(cv[:, :, 0:P], src[:, bass.ds(g * GT, GT), :]).then_inc(ctx_in.sem, 16)

        @block.gpsimd
        def _(pool):
            pool.memset(nv[:, :, P], 1.0)
            pool.memset(cv[:, :, P], 1.0)
            pool.memset(ebd[:, :, :, :].rearrange("p a b c -> p (a b c)"), 0.0).then_inc(cleared.sem, 1)
            with pool.Fori(0, NG) as g:
                norm.pool_part(pool, k, g)
                pool.wait_ge(ms_ready.sem, ms_ready.after(g))
                pool.tensor_tensor(r2[:, :], ms[:, :], k.neghalf[:, 0:GT], ALU.pow).then_inc(r2_ready.sem, 1)

        @block.vector
        def _(v):
            v.wait_ge(setup_in.sem, 16)
            v.wait_ge(cleared.sem, 1)
            v.memset(mx[:, :], 0.0).then_inc(x_updated.sem, 1)
            with v.Fori(0, NG) as g:
                x_t = lambda t: flat(k.x[:, bass.ds(g * GT + t, 1), :])
                norm.stats_part(v, chain, g, x_t)
                norm.scale_part(v, chain, g, x_t)
                chain.link(v, v.tensor_tensor(sq[:, :, :], xn[:, :, :], xn[:, :, :], ALU.mult), g)
                chain.link(v, v.tensor_reduce(ms[:, :], sq[:, :, :], AX.X, ALU.add), g)
                v.tensor_scalar(ms[:, :], ms[:, :], 1.0 / P, 1e-6, ALU.mult, ALU.add).then_inc(ms_ready.sem, 1)
                v.wait_ge(r2_ready.sem, r2_ready.after(g))
                for t in range(GT):
                    last = v.tensor_scalar(nv[:, t, 0:P], xn[:, t, :], r2[:, t:t + 1], None, ALU.mult)
                chain.link(v, last, g)
                v.tensor_tensor(nv[:, :, 0:P], nv[:, :, 0:P], bc(k.row("x1_nw"), 1, [P, GT, P]), ALU.mult).then_inc(n_ready.sem, 1)
                v.wait_ge(scores.sem, scores.after(g))
                chain.link(v, v.tensor_tensor(e[:, :, :, :].rearrange("p t a j -> p t (a j)"),
                                              S[:, :, :, :].rearrange("p t a j -> p t (a j)"),
                                              bc(flat(mask[:, :, :]), 1, [P, GT, P]), ALU.add), g)
                ev = e[:, :, :, :].rearrange("p t a j -> p t (a j)")
                chain.link(v, v.tensor_reduce(mx[:, :], ev, AX.X, ALU.max), g)
                v.tensor_tensor(ev, ev, bc(mx[:, :], 2, [P, GT, P]), ALU.subtract).then_inc(shifted.sem, 1)
                v.wait_ge(gate.sem, gate.after(g))
                v.tensor_tensor(z[:, :, :], PJ[:, 0, :].rearrange("p (t n) -> p t n", t=GT),
                                bc(k.row("x1_gb"), 1, [P, GT, P]), ALU.add).then_inc(z_ready.sem, 1)
                v.wait_ge(values.sem, values.after(g))
                av = AV[:, :, 0:2 * (P + 1)].rearrange("p a (b n) -> p a b n", b=2)
                chain.link(v, v.reciprocal(rs[:, :].rearrange("p (a b) -> p a b", a=2), av[:, :, :, P]), g)
                for t in range(GT):
                    last = v.scalar_tensor_tensor(hh[:, t, :], av[:, t // 2, t % 2, 0:P], rs[:, t:t + 1], xn[:, t, :],
                                                  ALU.mult, ALU.subtract)
                chain.link(v, last, g)
                v.wait_ge(alpha.sem, alpha.after(g))
                xg = k.x[:, bass.ds(g * GT, GT), :]
                v.tensor_tensor(xg, xg, xn[:, :, :], ALU.add)
                chain.link(v, v.scalar_tensor_tensor(hh[:, :, :], al[:, :, :], 1.0, hh[:, :, :], ALU.add, ALU.mult), g)
                v.scalar_tensor_tensor(xg, hh[:, :, :], 0.5, xg, ALU.mult, ALU.add).then_inc(x_updated.sem, 1)
                v.wait_ge(x_updated.sem, x_updated.after(g) + 1)
            chain.close()

        @block.scalar
        def _(act):
            act.wait_ge(cleared.sem, 1)
            with act.Fori(0, NG) as g:
                for n, dst in enumerate((nT, xT, cT)):
                    act.wait_ge(turned.sem, turned.after(g, n + 1))
                    act.copy(dst[:, :], PJ[:, n, :]).then_inc(turned_taken.sem, 1)
                for n, dst in enumerate((qT, kl, km)):
                    act.wait_ge(products.sem, products.after(g, n + 1))
                    act.mul(dst[:, :], PJ[:, n, :], float(P) ** -0.5 if n == 0 else 1.0).then_inc(products_taken.sem, 1)
                act.wait_ge(shifted.sem, shifted.after(g))
                for c in range(2):
                    rows = slice(64 * c, 64 * c + 64)
                    last = act.activation(ebd[rows, :, :, rows].rearrange("p t a j -> p (t a) j"),
                                          e[rows, :, :, :].rearrange("p t a j -> p (t a) j"), ACT.Exp)
                last.then_inc(weights.sem, 1)
                act.wait_ge(z_ready.sem, z_ready.after(g))
                act.activation(al[:, :, :], z[:, :, :], ACT.Tanh, scale=0.5).then_inc(alpha.sem, 1)
                for n in range(2):
                    act.wait_ge(w_turned.sem, w_turned.after(g, n + 1))
                    act.copy(eT[:, 2 * n:2 * n + 2, :, :].rearrange("p t a j -> p (t a j)"), TP[:, n, :]).then_inc(wT_ready.sem, 1)

        @block.tensor
        def _(pe):
            with pe.Fori(0, NG) as g:
                pe.wait_ge(n_ready.sem, n_ready.after(g))
                pe.wait_ge(x_updated.sem, x_updated.after(g))
                for t in range(GT):
                    last = pe.transpose(PJ[:, 0, P * t:P * t + P], nv[:, t, 0:P], k.ident[:, :])
                last.then_inc(turned.sem, 1)
                for t in range(GT):
                    last = pe.transpose(PJ[:, 1, P * t:P * t + P], xn[:, t, :], k.ident[:, :])
                last.then_inc(turned.sem, 1)
                pe.wait_ge(ctx_in.sem, ctx_in.after(g))
                for t in range(GT):
                    last = pe.transpose(PJ[:, 2, P * t:P * t + P], cv[:, t, 0:P], k.ident[:, :])
                last.then_inc(turned.sem, 1)
                for n, (w, src) in enumerate((("x1_q", nT), ("x1_k", nT), ("x1_k", cT))):
                    pe.wait_ge(turned_taken.sem, turned_taken.after(g, n + 1))
                    pe.matmul(PJ[:, n, :], k.mat(w), src[:, :], start=True, stop=True).then_inc(products.sem, 1)
                pe.wait_ge(products_taken.sem, products_taken.after(g, 3))
                for b in range(2 * GT):
                    c, t = b % 2, b // 2
                    tok = slice(SL * b, SL * b + SL)
                    for a, keys in enumerate((kl, km)):
                        last = pe.matmul(S[64 * c:64 * c + 64, t, a, :], qT[:, tok], keys[:, tok], start=True, stop=True)
                last.then_inc(scores.sem, 1)
                for t in range(GT):
                    last = pe.matmul(PJ[:, 0, P * t:P * t + P], xT[:, P * t:P * t + P], k.mat("x1_g"), start=True, stop=True)
                last.then_inc(gate.sem, 1)
                pe.wait_ge(weights.sem, weights.after(g))
                for n in range(2):
                    for i in range(4):
                        last = pe.transpose(TP[:, n, P * i:P * i + P], ebd[:, 2 * n + i // 2, i % 2, :], k.ident[:, :])
                    last.then_inc(w_turned.sem, 1)
                for t in range(GT):
                    if t % 2 == 0:
                        pe.wait_ge(wT_ready.sem, wT_ready.after(g, t // 2 + 1))
                    out = AV[:, t // 2, (P + 1) * (t % 2):(P + 1) * (t % 2) + P + 1]
                    pe.matmul(out, eT[:, t, 0, :], nv[:, t, :], start=True, stop=False)
                    last = pe.matmul(out, eT[:, t, 1, :], cv[:, t, :], start=False, stop=True)
                last.then_inc(values.sem, 1)
    ph.close()



def pooling(nc, k, d, tag):
    ph = Phase(nc, tag)
    norm, norm2 = Norm(ph), Norm(ph, "ln2")
    tri, inv = ph.sb("tri", [P, P]), ph.sb("inv", [P, 1])
    hT, qT, mT = ph.sb("hT", [P, GN]), ph.sb("qT", [P, GN]), ph.sb("mT", [P, GN])
    qkv = ph.sb("qkv", [P, GT, 3 * P])
    l, e, w = ph.sb("l", [P, GT, P]), ph.sb("e", [P, GT, P]), ph.sb("w", [P, GT, P])
    mixed = ph.sb("mixed", [P, GT, P])
    mx, rs = ph.sb("mx", [P, GT]), ph.sb("rs", [P, GT])
    PJ, QKV = ph.ps("PJ", [P, 3, 512]), ph.ps("QKV", [P, GT, 512])
    setup_in = ph.counter("setup_in")
    turned, hT_ready, qkv_product, q_product = ph.counter("turned"), ph.counter("hT_ready"), ph.counter("qkv_product"), ph.counter("q_product")
    qT_ready, mixed_ready, m_turned, mT_ready = ph.counter("qT_ready"), ph.counter("mixed_ready"), ph.counter("m_turned"), ph.counter("mT_ready")
    logits, shifted, weights = ph.counter("logits", 2), ph.counter("shifted", 2), ph.counter("weights", 2)
    summands, sums, x_updated = ph.counter("summands", 2), ph.counter("sums", 2), ph.counter("x_updated")
    chain = ph.links("dve_chain")
    INV = float(P) ** -0.5
    with nc.Block() as block:
        @block.sync
        def _(sp):
            sp.dma_start(tri[:, :], d["tri_seq"]).then_inc(setup_in.sem, 16)
            sp.dma_start(inv[:, :], d["inv_count"]).then_inc(setup_in.sem, 16)
            load_experts(sp, k, d, "f3", 8, k.f3_in)

        @block.gpsimd
        def _(pool):
            with pool.Fori(0, NG) as g:
                norm.pool_part(pool, k, g)
                norm2.pool_part(pool, k, g)

        @block.vector
        def _(v):
            v.wait_ge(setup_in.sem, 32)
            v.memset(mx[:, :], 0.0).then_inc(x_updated.sem, 1)
            grp = lambda ap: ap.rearrange("p (t n) -> p t n", t=GT)

            def norms(g):
                x_t = lambda t: flat(k.x[:, bass.ds(g * GT + t, 1), :])
                norm.stats_part(v, chain, g, x_t)
                norm.scale_part(v, chain, g, x_t)
                xn_t = lambda t: norm.xn[:, t, :]
                norm2.stats_part(v, chain, g, xn_t)
                norm2.scale_part(v, chain, g, xn_t)

            def body(g, last_group):
                v.wait_ge(qkv_product.sem, qkv_product.after(g))
                bias = k.rows[:, ROWS.index("a2_bq"):ROWS.index("a2_bq") + 3, :].rearrange("p a n -> p (a n)")
                chain.link(v, v.tensor_tensor(qkv[:, :, :], QKV[:, :, 0:3 * P], bc(bias, 1, [P, GT, 3 * P]), ALU.add))
                for n, row in enumerate(("a2_bqa", "a2_bka")):
                    src = qkv[:, :, 0:P] if n == 0 else mixed[:, :, :]
                    v.wait_ge(logits.sem, logits.after(g, n + 1))
                    chain.link(v, v.tensor_tensor(l[:, :, :], grp(PJ[:, 1, :]), bc(k.row(row), 1, [P, GT, P]), ALU.add))
                    chain.link(v, v.tensor_reduce(mx[:, :], l[:, :, :], AX.X, ALU.max))
                    v.tensor_tensor(l[:, :, :], l[:, :, :], bc(mx[:, :], 2, [P, GT, P]), ALU.subtract).then_inc(shifted.sem, 1)
                    v.wait_ge(weights.sem, weights.after(g, n + 1))
                    v.tensor_tensor(w[:, :, :], e[:, :, :], src, ALU.mult)
                    chain.link(v, v.tensor_reduce(rs[:, :], e[:, :, :], AX.X, ALU.add))
                    chain.link(v, v.reciprocal(rs[:, :], rs[:, :]))
                    v.tensor_tensor(w[:, :, :], w[:, :, :], bc(rs[:, :], 2, [P, GT, P]), ALU.mult).then_inc(summands.sem, 1)
                    v.wait_ge(sums.sem, sums.after(g, n + 1))
                    if n == 0:
                        ins = v.scalar_tensor_tensor(mixed[:, :, :], grp(PJ[:, 2, :]), inv[:, 0:1], qkv[:, :, P:2 * P], ALU.mult, ALU.mult)
                        ins.then_inc(mixed_ready.sem, 1)
                        v.wait_ge(mixed_ready.sem, mixed_ready.after(g))
                        if not last_group:
                            norms(g + 1)
                    else:
                        chain.link(v, v.scalar_tensor_tensor(l[:, :, :], grp(PJ[:, 2, :]), inv[:, 0:1], qkv[:, :, 2 * P:3 * P],
                                                             ALU.mult, ALU.mult))
                xg = k.x[:, bass.ds(g * GT, GT), :]
                v.tensor_tensor(xg, xg, l[:, :, :], ALU.add).then_inc(x_updated.sem, 1)
                v.wait_ge(x_updated.sem, x_updated.after(g) + 1)

            norms(0)
            with v.Fori(0, NG - 1) as g:
                chain.enter(g, 14)
                body(g, False)
            chain.leave(NG - 1)
            body(NG - 1, True)

        @block.scalar
        def _(act):
            with act.Fori(0, NG) as g:
                act.wait_ge(turned.sem, turned.after(g))
                act.activation(hT[:, :], PJ[:, 0, :], ACT.Identity, bias=k.col("a2_be"), scale=k.col("a2_ga")).then_inc(hT_ready.sem, 1)
                act.wait_ge(q_product.sem, q_product.after(g))
                act.activation(qT[:, :], PJ[:, 0, :], ACT.Identity, bias=k.col("a2_bq")).then_inc(qT_ready.sem, 1)
                for n in range(2):
                    if n:
                        act.wait_ge(m_turned.sem, m_turned.after(g))
                        act.copy(mT[:, :], PJ[:, 0, :]).then_inc(mT_ready.sem, 1)
                    act.wait_ge(shifted.sem, shifted.after(g, n + 1))
                    act.activation(e[:, :, :], l[:, :, :], ACT.Exp, scale=INV).then_inc(weights.sem, 1)

        @block.tensor
        def _(pe):
            pe.wait_ge(setup_in.sem, 32)
            with pe.Fori(0, NG) as g:
                pe.wait_ge(norm2.xn_ready.sem, norm2.xn_ready.after(g))
                pe.wait_ge(x_updated.sem, x_updated.after(g))
                for t in range(GT):
                    last = pe.transpose(PJ[:, 0, P * t:P * t + P], norm2.xn[:, t, :], k.ident[:, :])
                last.then_inc(turned.sem, 1)
                pe.wait_ge(hT_ready.sem, hT_ready.after(g))
                pe.matmul(PJ[:, 0, :], k.mat("a2_q"), hT[:, :], start=True, stop=True).then_inc(q_product.sem, 1)
                m0 = MATS.index("a2_q")
                for t in range(GT):
                    last = pe.matmul(QKV[:, t, 0:3 * P], hT[:, P * t:P * t + P], flat(k.mats[:, m0:m0 + 3, :]), start=True, stop=True)
                last.then_inc(qkv_product.sem, 1)
                for n, (src, mat) in enumerate(((qT, "a2_qa"), (mT, "a2_ka"))):
                    if n == 0:
                        pe.wait_ge(qT_ready.sem, qT_ready.after(g))
                    else:
                        pe.wait_ge(mixed_ready.sem, mixed_ready.after(g))
                        for t in range(GT):
                            last = pe.transpose(PJ[:, 0, P * t:P * t + P], mixed[:, t, :], k.ident[:, :])
                        last.then_inc(m_turned.sem, 1)
                        pe.wait_ge(mT_ready.sem, mT_ready.after(g))
                    for t in range(GT):
                        last = pe.matmul(PJ[:, 1, P * t:P * t + P], src[:, P * t:P * t + P], k.mat(mat), start=True, stop=True)
                    last.then_inc(logits.sem, 1)
                    pe.wait_ge(summands.sem, summands.after(g, n + 1))
                    pe.matmul(PJ[:, 2, :], tri[:, :], w[:, :, :], start=True, stop=True).then_inc(sums.sem, 1)
    ph.close()



def ternary(nc, k, d, tag):
    ph = Phase(nc, tag)
    norm = Norm(ph)
    w = ph.sb("w", [P, 2, 512])
    b1, ones = ph.sb("b1", [P, 4]), ph.sb("ones", [P, P])
    ab, gm = ph.sb("ab", [P, 2]), ph.sb("gm", [P, 2])
    xT, h = ph.sb("xT", [P, GN]), ph.sb("h", [P, 4, GN])
    PJ, H, Y, G = ph.ps("PJ", [P, 512]), ph.ps("H", [P, 4, 512]), ph.ps("Y", [P, 512]), ph.ps("G", [P, 2])
    setup_in, ones_made, abs_ready, gamma_sum, ternary_ready = (ph.counter(n) for n in (
        "setup_in", "ones_made", "abs_ready", "gamma_sum", "ternary_ready"))
    x_transposed, xT_ready, product, x_updated = (ph.counter(n) for n in ("x_transposed", "xT_ready", "product", "x_updated"))
    hidden, h_ready = ph.counter("hidden", 4), ph.counter("h_ready", 4)
    st, chain = ph.chain("setup_chain", 0), ph.links("dve_chain")
    MAGIC = 1.5 * 2.0 ** 23
    with nc.Block() as block:
        @block.sync
        def _(sp):
            sp.dma_start(flat(w[:, :, :]), d["f2_w"]).then_inc(setup_in.sem, 16)
            sp.dma_start(b1[:, :], d["f2_b1"]).then_inc(setup_in.sem, 16)

        @block.gpsimd
        def _(pool):
            pool.memset(ones[:, :], 1.0).then_inc(ones_made.sem, 1)
            with pool.Fori(0, NG) as g:
                norm.pool_part(pool, k, g)

        @block.vector
        def _(v):
            v.wait_ge(setup_in.sem, 32)
            v.tensor_reduce(ab[:, :], w[:, :, :], AX.X, ALU.add, apply_absolute_value=True).then_inc(abs_ready.sem, 1)
            v.wait_ge(gamma_sum.sem, 1)
            st.link(v, v.tensor_scalar(gm[:, :], G[:, :], 1.0 / (P * 512), 1e-5, ALU.mult, ALU.add))
            st.link(v, v.reciprocal(gm[:, :], gm[:, :]))
            for n in range(2):
                last = v.tensor_scalar(w[:, n, :], w[:, n, :], gm[:, n:n + 1], MAGIC, ALU.mult, ALU.add)
            st.link(v, last)
            st.link(v, v.tensor_scalar(w[:, :, :], w[:, :, :], MAGIC, 1.0, ALU.subtract, ALU.min))
            v.tensor_scalar(w[:, :, :], w[:, :, :], -1.0, None, ALU.max).then_inc(ternary_ready.sem, 1)
            v.memset(ab[:, :], 0.0).then_inc(x_updated.sem, 1)

            def norm_group(g, first):
                x_t = lambda t: flat(k.x[:, bass.ds(g * GT + t, 1), :])
                norm.stats_part(v, chain, g, x_t)
                if not first:
                    v.wait_ge(x_transposed.sem, x_transposed.after(g - 1))
                norm.scale_part(v, chain, g, x_t)

            def update(g):
                xg = k.x[:, bass.ds(g * GT, GT), :]
                chain.link(v, v.tensor_tensor(xg, xg, bc(k.row("f2_b2"), 1, [P, GT, P]), ALU.add))
                v.wait_ge(product.sem, product.after(g))
                v.tensor_tensor(xg, xg, Y[:, :].rearrange("p (t n) -> p t n", t=GT), ALU.add).then_inc(x_updated.sem, 1)
                v.wait_ge(x_updated.sem, x_updated.after(g) + 1)

            norm_group(0, True)
            with v.Fori(1, NG) as g:
                chain.enter(g - 1, 3)
                norm_group(g, False)
                update(g - 1)
            chain.leave(NG - 1)
            update(NG - 1)

        @block.scalar
        def _(act):
            act.wait_ge(setup_in.sem, 32)
            with act.Fori(0, NG) as g:
                act.wait_ge(x_transposed.sem, x_transposed.after(g))
                act.copy(xT[:, :], PJ[:, :]).then_inc(xT_ready.sem, 1)
                for c in range(4):
                    act.wait_ge(hidden.sem, hidden.after(g, c + 1))
                    act.activation(h[:, c, :], H[:, c, :], ACT.Relu, bias=b1[:, c:c + 1]).then_inc(h_ready.sem, 1)

        @block.tensor
        def _(pe):
            pe.wait_ge(ones_made.sem, 1)
            pe.wait_ge(abs_ready.sem, 1)
            pe.matmul(G[:, :], ones[:, :], ab[:, :], start=True, stop=True).then_inc(gamma_sum.sem, 1)
            pe.wait_ge(ternary_ready.sem, 1)
            with pe.Fori(0, NG) as g:
                pe.wait_ge(norm.xn_ready.sem, norm.xn_ready.after(g))
                for t in range(GT):
                    last = pe.transpose(PJ[:, P * t:P * t + P], norm.xn[:, t, :], k.ident[:, :])
                last.then_inc(x_transposed.sem, 1)
                pe.wait_ge(xT_ready.sem, xT_ready.after(g))
                for c in range(4):
                    pe.matmul(H[:, c, :], w[:, 0, P * c:P * c + P], xT[:, :], start=True, stop=True).then_inc(hidden.sem, 1)
                pe.wait_ge(h_ready.sem, h_ready.after(g))
                pe.wait_ge(x_updated.sem, x_updated.after(g))
                for t in range(GT):
                    for c in range(4):
                        last = pe.matmul(Y[:, P * t:P * t + P], h[:, c, P * t:P * t + P], w[:, 1, P * c:P * c + P],
                                         start=c == 0, stop=c == 3)
                last.then_inc(product.sem, 1)
    ph.close()



def experts(nc, k, d, tag, shared):
    ph = Phase(nc, tag)
    E = 8
    NE = E + (1 if shared else 0)
    CAP = max(8, int(max(1, NB * SL * 2 // E) * 1.25))
    F = 4
    norm = Norm(ph)
    router, rb = ph.sb("router", [P, E]), ph.sb("rb", [P, E])
    b1, b2 = ph.sb("b1", [P, NE * F]), ph.sb("b2", [NE, P])
    tri, ones, low = ph.sb("tri", [P, P]), ph.sb("ones", [P, P]), ph.sb("low", [P, E, E])
    xT, xTall = ph.sb("xT", [P, GN]), ph.sb("xTall", [P, NG, GN])
    lg = ph.sb("lg", [P, NT, E])
    wts = ph.sb("wts", [P, NT, NE])
    ws, wT = ph.sb("ws", [P, GT, NE]), ph.sb("wT", [NE, GN])
    small = [P, NT, E]
    PJ, LG = ph.ps("PJ", [P, 512]), ph.ps("LG", [P, 512])
    H, Y = ph.ps("H", [P, 4, 512]), ph.ps("Y", [P, 2, 512])
    setup_in, ones_made = ph.counter("setup_in"), ph.counter("ones_made")
    x_transposed, xT_ready, logits, logits_taken = (ph.counter(n) for n in ("x_transposed", "xT_ready", "logits", "logits_taken"))
    top_ready, exp_ready, picked, counted_in_tile, counted_tiles, wts_ready = (ph.counter(n) for n in (
        "top_ready", "exp_ready", "picked", "counted_in_tile", "counted_tiles", "wts_ready"))
    ws_ready, w_turned, wT_ready = ph.counter("ws_ready"), ph.counter("w_turned"), ph.counter("wT_ready")
    hidden, h_ready = ph.counter("hidden", NE * F), ph.counter("h_ready", NE * F)
    out, taken = ph.counter("out", NE + 1), ph.counter("taken", NE + 1)
    chain, st = ph.links("dve_chain"), ph.chain("routing", 0)
    weights_in = k.f1_in if shared else k.f3_in
    w1 = k.moe[:, 0:NE * 512].rearrange("p (e n) -> p e n", e=NE)
    w2 = k.moe[:, NE * 512:2 * NE * 512].rearrange("p (e c n) -> p e c n", e=NE, c=F)
    scr = ExitStack()
    t1 = scr.enter_context(nc.sbuf_tensor(f"{tag}_t1", [P, NT, E, E], F32))
    t2 = scr.enter_context(nc.sbuf_tensor(f"{tag}_t2", [P, NT, E, E], F32))
    p1 = scr.enter_context(nc.sbuf_tensor(f"{tag}_p1", small, F32))
    sel = scr.enter_context(nc.sbuf_tensor(f"{tag}_sel", small, F32))
    tot = scr.enter_context(nc.sbuf_tensor(f"{tag}_tot", small, F32))
    run = scr.enter_context(nc.sbuf_tensor(f"{tag}_run", small, F32))
    zz = scr.enter_context(nc.sbuf_tensor(f"{tag}_zz", [P, NT], F32))
    m1, s1 = (scr.enter_context(nc.sbuf_tensor(f"{tag}_{n}", [P, NT], F32)) for n in ("m1", "s1"))
    scr.close()
    h = ph.sb("h", [P, 2, F, GN])
    if True:
        with nc.Block() as block:
            @block.sync
            def _(sp):
                for dst, name in ((router[:, :], "router"), (rb[:, :], "rb"), (b1[:, :], "b1"), (b2[:, :], "b2")):
                    sp.dma_start(dst, d[f"{tag}_{name}"]).then_inc(setup_in.sem, 16)
                sp.dma_start(tri[:, :], d["tri_all"]).then_inc(setup_in.sem, 16)
                sp.dma_start(flat(low[:, :, :]), d["low"]).then_inc(setup_in.sem, 16)

            @block.gpsimd
            def _(pool):
                pool.memset(ones[:, :], 1.0).then_inc(ones_made.sem, 1)
                with pool.Fori(0, NG) as g:
                    norm.pool_part(pool, k, g)

            @block.vector
            def _(v):
                v.wait_ge(setup_in.sem, 96)
                v.memset(zz[:, :], 0.0)
                v.memset(wts[:, :, :], 1.0).then_inc(logits_taken.sem, 1)

                def norm_group(g, first):
                    x_t = lambda t: flat(k.x[:, bass.ds(g * GT + t, 1), :])
                    norm.stats_part(v, chain, g, x_t)
                    if not first:
                        v.wait_ge(x_transposed.sem, x_transposed.after(g - 1))
                    norm.scale_part(v, chain, g, x_t)
                    if shared:
                        xg = k.x[:, bass.ds(g * GT, GT), :]
                        v.tensor_tensor(xg, xg, norm.xn[:, :, :], ALU.add)

                def take_logits(g):
                    v.wait_ge(logits.sem, logits.after(g))
                    v.tensor_tensor(lg[:, bass.ds(g * GT, GT), :], LG[:, 0:GT * E].rearrange("p (t e) -> p t e", e=E),
                                    bc(rb[:, :], 1, [P, GT, E]), ALU.add).then_inc(logits_taken.sem, 1)
                    v.wait_ge(logits_taken.sem, logits_taken.after(g) + 1)

                norm_group(0, True)
                with v.Fori(1, NG) as g:
                    chain.enter(g - 1, 2)
                    norm_group(g, False)
                    take_logits(g - 1)
                chain.leave(NG - 1)
                take_logits(NG - 1)
                st.link(v, v.tensor_reduce(m1[:, :], lg[:, :, :], AX.X, ALU.max))
                v.tensor_tensor(p1[:, :, :], lg[:, :, :], bc(m1[:, :], 2, small), ALU.subtract).then_inc(top_ready.sem, 1)
                v.wait_ge(exp_ready.sem, 1)
                rank = lg
                if shared:
                    rank = p1
                    st.link(v, v.tensor_reduce(s1[:, :], p1[:, :, :], AX.X, ALU.add))
                    st.link(v, v.reciprocal(s1[:, :], s1[:, :]))
                    st.link(v, v.tensor_tensor(p1[:, :, :], p1[:, :, :], bc(s1[:, :], 2, small), ALU.mult))
                wide = [P, NT, E, E]
                mine, other = bc(rank[:, :, :], 3, wide), bc(rank[:, :, :], 2, wide)
                v.tensor_tensor(t1[:, :, :, :], other, mine, ALU.is_gt)
                st.link(v, v.tensor_tensor(t2[:, :, :, :], other, mine, ALU.is_equal))
                t2v = t2[:, :, :, :].rearrange("p t a b -> p t (a b)")
                st.link(v, v.tensor_tensor(t2v, t2v, bc(flat(low[:, :, :]), 1, [P, NT, E * E]), ALU.mult))
                st.link(v, v.tensor_tensor(t1[:, :, :, :], t1[:, :, :, :], t2[:, :, :, :], ALU.add))
                st.link(v, v.tensor_reduce(sel[:, :, :], t1[:, :, :, :], AX.X, ALU.add))
                ins = v.tensor_scalar(sel[:, :, :], sel[:, :, :], 2.0, None, ALU.is_lt)
                ins.then_inc(picked.sem, 1)
                v.wait_ge(picked.sem, 1)
                st.link(v, v.tensor_tensor(p1[:, :, :], p1[:, :, :], sel[:, :, :], ALU.mult))
                st.link(v, v.tensor_reduce(s1[:, :], p1[:, :, :], AX.X, ALU.add))
                if shared:
                    st.link(v, v.tensor_scalar(s1[:, :], s1[:, :], 1e-9, None, ALU.add))
                st.link(v, v.reciprocal(s1[:, :], s1[:, :]))
                ins = v.tensor_tensor(wts[:, :, 0:E], p1[:, :, :], bc(s1[:, :], 2, small), ALU.mult)
                if not shared:
                    st.link(v, ins)
                    v.wait_ge(counted_tiles.sem, 1)
                    st.link(v, v.tensor_copy(flat(tot[:, :, :]), Y[:, 1, 0:NT * E]))
                    for x in range(E):
                        last = v.tensor_tensor_scan(run[:, :, x], tot[:, :, x], zz[:, :], 0.0, ALU.add, ALU.add)
                    st.link(v, last)
                    st.link(v, v.tensor_tensor(run[:, :, :], run[:, :, :], tot[:, :, :], ALU.subtract))
                    st.link(v, v.tensor_tensor(flat(run[:, :, :]), flat(run[:, :, :]), Y[:, 0, 0:NT * E], ALU.add))
                    st.link(v, v.tensor_scalar(run[:, :, :], run[:, :, :], float(CAP), None, ALU.is_le))
                    ins = v.tensor_tensor(wts[:, :, :], wts[:, :, :], run[:, :, :], ALU.mult)
                ins.then_inc(wts_ready.sem, 1)
                v.wait_ge(wts_ready.sem, 1)
                v.memset(norm.var[:, :], 0.0).then_inc(taken.sem, 2)
                with v.Fori(0, NG) as g:
                    v.tensor_copy(ws[:, :, :], wts[:, bass.ds(g * GT, GT), :]).then_inc(ws_ready.sem, 1)
                    v.wait_ge(w_turned.sem, w_turned.after(g))
                    v.tensor_copy(wT[:, :], LG[0:NE, :]).then_inc(wT_ready.sem, 1)
                    for x in range(NE):
                        v.wait_ge(out.sem, out.after(g, x + 1))
                        for t in range(GT):
                            xt = flat(k.x[:, bass.ds(g * GT + t, 1), :])
                            wt = flat(wts[:, bass.ds(g * GT + t, 1), :])[:, x:x + 1]
                            last = v.scalar_tensor_tensor(xt, Y[:, x % 2, P * t:P * t + P], wt, xt, ALU.mult, ALU.add)
                        last.then_inc(taken.sem, 1)
                        v.wait_ge(taken.sem, taken.after(g, x + 1) + 2)
                    v.wait_ge(out.sem, out.after(g))
                    xg = k.x[:, bass.ds(g * GT, GT), :]
                    v.tensor_tensor(xg, xg, Y[:, NE % 2, :].rearrange("p (t n) -> p t n", t=GT), ALU.add).then_inc(taken.sem, 1)
                    v.wait_ge(taken.sem, taken.after(g) + 2)

            @block.scalar
            def _(act):
                act.wait_ge(setup_in.sem, 96)
                with act.Fori(0, NG) as g:
                    act.wait_ge(x_transposed.sem, x_transposed.after(g))
                    act.copy(flat(xTall[:, bass.ds(g, 1), :]), PJ[:, :])
                    act.copy(xT[:, :], PJ[:, :]).then_inc(xT_ready.sem, 1)
                act.wait_ge(top_ready.sem, 1)
                act.activation(p1[:, :, :], p1[:, :, :], ACT.Exp).then_inc(exp_ready.sem, 1)
                act.wait_ge(wts_ready.sem, 1)
                with act.Fori(0, NG) as g:
                    for x in range(NE):
                        for c in range(F):
                            n = x * F + c
                            act.wait_ge(hidden.sem, hidden.after(g, n + 1))
                            act.activation(h[:, x % 2, c, :], H[:, c, :], ACT.Gelu_apprx_tanh, bias=b1[:, n:n + 1])\
                                .then_inc(h_ready.sem, 1)

            @block.tensor
            def _(pe):
                pe.wait_ge(setup_in.sem, 96)
                with pe.Fori(0, NG) as g:
                    pe.wait_ge(norm.xn_ready.sem, norm.xn_ready.after(g))
                    for t in range(GT):
                        last = pe.transpose(PJ[:, P * t:P * t + P], norm.xn[:, t, :], k.ident[:, :])
                    last.then_inc(x_transposed.sem, 1)
                    pe.wait_ge(xT_ready.sem, xT_ready.after(g))
                    pe.wait_ge(logits_taken.sem, logits_taken.after(g))
                    for t in range(GT):
                        last = pe.matmul(LG[:, E * t:E * t + E], xT[:, P * t:P * t + P], router[:, :], start=True, stop=True)
                    last.then_inc(logits.sem, 1)
                if not shared:
                    pe.wait_ge(ones_made.sem, 1)
                    pe.wait_ge(picked.sem, 1)
                    pe.matmul(Y[:, 0, 0:NT * E], tri[:, :], sel[:, :, :], start=True, stop=True)
                    pe.matmul(Y[:, 1, 0:NT * E], ones[:, :], sel[:, :, :], start=True, stop=True).then_inc(counted_tiles.sem, 1)
                pe.wait_ge(weights_in, 32)
                pe.wait_ge(wts_ready.sem, 1)
                with pe.Fori(0, NG) as g:
                    xg = flat(xTall[:, bass.ds(g, 1), :])

                    def make_hidden(x):
                        for c in range(F):
                            pe.matmul(H[:, c, :], w1[:, x, P * c:P * c + P], xg, start=True, stop=True).then_inc(hidden.sem, 1)

                    make_hidden(0)
                    pe.wait_ge(ws_ready.sem, ws_ready.after(g))
                    for t in range(GT):
                        last = pe.transpose(LG[0:NE, P * t:P * t + P], ws[:, t, :], k.ident[:, :])
                    last.then_inc(w_turned.sem, 1)
                    for x in range(NE):
                        pe.wait_ge(h_ready.sem, h_ready.after(g, F * (x + 1)))
                        if x + 1 < NE:
                            make_hidden(x + 1)
                        pe.wait_ge(taken.sem, g * (NE + 1) + (x + 1 if x else 2))
                        for t in range(GT):
                            for c in range(F):
                                last = pe.matmul(Y[:, x % 2, P * t:P * t + P], h[:, x % 2, c, P * t:P * t + P], w2[:, x, c, :],
                                                 start=c == 0, stop=c == F - 1)
                        last.then_inc(out.sem, 1)
                    pe.wait_ge(wT_ready.sem, wT_ready.after(g))
                    pe.wait_ge(taken.sem, g * (NE + 1) + NE + 1)
                    for t in range(GT):
                        last = pe.matmul(Y[:, NE % 2, P * t:P * t + P], wT[:, P * t:P * t + P], b2[:, :], start=True, stop=True)
                    last.then_inc(out.sem, 1)
    ph.close()



def shape_tables():
    import numpy as np
    f = np.float32
    p = np.arange(P)
    t = {}
    t["ident"] = np.eye(P, dtype=f)
    t["mask4"] = ((p[:, None] // 8) % 4 == np.arange(4)[None, :]).astype(f) * f(8.0 ** -0.5)
    t["causal"] = np.where(np.arange(SL)[None, :] > (p[:, None] % SL), f(NEG), f(0)).astype(f)
    n, s = SL, 32
    pos = np.arange(n, dtype=f) * f((s - 1) / (n - 1))
    i0 = np.floor(pos).astype(np.int32)
    i1 = np.minimum(i0 + 1, s - 1)
    frac = (pos - i0.astype(f)).astype(f)
    m = np.zeros((n, s), f)
    np.add.at(m, (np.arange(n), i0), f(1) - frac)
    np.add.at(m, (np.arange(n), i1), frac)
    m[-1] = 0
    t["mask2"] = np.concatenate([t["causal"], np.zeros((P, SL), f)], axis=1)
    same = p[:, None] // SL == p[None, :] // SL
    t["tri_all"] = (p[:, None] <= p[None, :]).astype(f)
    t["tri_seq"] = ((p[:, None] <= p[None, :]) & same).astype(f)
    t["inv_count"] = (f(1) / (p % SL + 1).astype(f)).reshape(P, 1)
    t["low"] = np.broadcast_to((np.arange(8)[None, :] < np.arange(8)[:, None]).astype(f).reshape(1, 64), (P, 64))
    leaf = np.zeros((96, 24, P), np.uint16)
    for n in range(24):
        for j in range(P):
            leaf[32 * (n // 8) + (n % 8 * P + j) // 64, n, j] = 0x3F80
    t["leaf"] = leaf.reshape(96, 24 * P)
    t["interpT"] = np.ascontiguousarray(np.concatenate([m.T, m.T, m.T], axis=1))
    return t


def lay_out(inp):
    import numpy as np
    i = {n: np.asarray(a) for n, a in inp.items()}
    f = np.float32
    d = dict(shape_tables())
    d["x"] = i["x"].reshape(NB * SL, P)
    d["ctx"] = i["ctx_1024"].reshape(NB * SL, P)
    qkv = i["L1_attn_Wqkv"].reshape(P, NH, 3, 8)
    bqkv = i["L1_attn_bqkv"].reshape(NH, 3, 8)

    def grouped(w):
        z = np.zeros((P, P), f)
        for g in range(4):
            z[32 * g:32 * g + 32, 32 * g:32 * g + 32] = w[g]
        return z

    mats = {"a0_q": i["L0_attn_Wq"], "a0_k": i["L0_attn_Wk"], "a0_v": i["L0_attn_Wv"], "a0_o": i["L0_attn_Wo"],
            "a1_q": qkv[:, :, 0].reshape(P, P), "a1_k": qkv[:, :, 1].reshape(P, P), "a1_v": qkv[:, :, 2].reshape(P, P),
            "a1_o": i["L1_attn_Wout"],
            "x1_q": i["L1_xattn_q_w"].T, "x1_k": i["L1_xattn_k_w"].T, "x1_g": i["L1_xattn_gate_w"].T,
            "a2_q": i["L2_attn_Wq"], "a2_k": i["L2_attn_Wk"], "a2_v": i["L2_attn_Wv"],
            "a2_qa": i["L2_attn_Wqa"], "a2_ka": i["L2_attn_Wka"],
            "x2_q": i["L2_xattn_wq"].T, "x2_k": i["L2_xattn_wk"].T, "x2_v": i["L2_xattn_wv"].T, "x2_o": i["L2_xattn_wo"].T,
            "a3_q": i["L3_attn_Wq"].T, "a3_k": i["L3_attn_Wk"].T, "a3_v": i["L3_attn_Wv"].T, "a3_o": i["L3_attn_Wo"].T,
            "x3_q": grouped(i["L3_xattn_wq"]), "x3_k": grouped(i["L3_xattn_wk"]), "x3_v": grouped(i["L3_xattn_wv"])}
    d["mats"] = np.concatenate([mats[n] for n in MATS], axis=1)
    cols = {"a1_bq": bqkv[:, 0].reshape(P), "a1_bk": bqkv[:, 1].reshape(P), "x1_nw": i["L1_xattn_norm_w"],
            "a2_ga": i["L2_attn_gamma"], "a2_be": i["L2_attn_beta"], "a2_bq": i["L2_attn_bq"],
            "x2_bq": i["L2_xattn_bq"], "x2_bk": i["L2_xattn_bk"], "a3_bq": i["L3_attn_bq"], "a3_bk": i["L3_attn_bk"],
            "a3_ga": i["L3_attn_gamma"], "a3_be": i["L3_attn_beta"], "x3_bq": i["L3_xattn_bq"], "x3_bk": i["L3_xattn_bk"]}
    d["cols"] = np.stack([cols[n] for n in COLS], axis=1)
    rows = {"a0_g": np.tile(i["L0_attn_ln_g"], 8), "a0_b": np.tile(i["L0_attn_ln_b"], 8),
            "a1_bv": bqkv[:, 2].reshape(P), "a1_bo": i["L1_attn_bout"], "x1_gb": i["L1_xattn_gate_b"],
            "x1_nw": i["L1_xattn_norm_w"], "a2_bq": i["L2_attn_bq"], "a2_bk": i["L2_attn_bk"], "a2_bv": i["L2_attn_bv"],
            "a2_bqa": i["L2_attn_bqa"], "a2_bka": i["L2_attn_bka"], "x2_bv": i["L2_xattn_bv"], "x2_bo": i["L2_xattn_bo"],
            "a3_bv": i["L3_attn_bv"], "a3_bo": i["L3_attn_bo"], "x3_bv": i["L3_xattn_bv"], "f2_b2": i["L2_ffn_b2"]}
    rep = lambda a: np.ascontiguousarray(np.broadcast_to(a.reshape(1, -1), (P, a.size)))
    d["rows"] = rep(np.concatenate([rows[n] for n in ROWS]))
    d["lq"] = rep(np.concatenate([i["L0_attn_lq1"], i["L0_attn_lk1"], i["L0_attn_lq2"], i["L0_attn_lk2"]]))
    d["relT"] = np.ascontiguousarray(i["L3_attn_rel_bias"].transpose(2, 0, 1)).reshape(32, NH * 32)

    def chunks(w):
        w = w.reshape(-1, P, w.shape[-1])
        return w.transpose(1, 0, 2).reshape(P, -1)

    t3 = [{n: i[f"L0_ffn_{t}_{n}"] for n in ("node_w", "node_b", "w1", "b1", "w2", "b2")} for t in "qkv"]
    d["f0_nodes"] = np.concatenate([t["node_w"].T for t in t3], axis=1)
    d["f0_nodeb"] = rep(np.concatenate([t["node_b"] for t in t3]))
    d["f0_b1"] = np.concatenate([t["b1"].reshape(8, P).T for t in t3], axis=1)
    b2 = np.zeros((96, 3, P), f)
    for r in range(3):
        b2[32 * r:32 * r + 16, r] = t3[r]["b2"]
    d["f0_b2"] = b2.reshape(96, 3 * P)
    d["f0_w1"] = np.concatenate([t["w1"].transpose(1, 0, 2).reshape(P, -1) for t in t3], axis=1)
    d["f0_w2"] = np.concatenate([chunks(t["w2"].reshape(1024, P)) for t in t3], axis=1)
    d["f2_w"] = np.concatenate([i["L2_ffn_W1"].T, chunks(i["L2_ffn_W2"].T)], axis=1)
    d["f2_b1"] = i["L2_ffn_b1"].reshape(4, P).T
    d["f1_w1"] = np.concatenate([i["L1_ffn_ew1"].transpose(1, 0, 2).reshape(P, -1), i["L1_ffn_sh_w1"]], axis=1)
    d["f1_w2"] = np.concatenate([chunks(i["L1_ffn_ew2"]), chunks(i["L1_ffn_sh_w2"])], axis=1)
    d["f1_b1"] = np.concatenate([i["L1_ffn_eb1"].reshape(32, P).T, i["L1_ffn_sh_b1"].reshape(4, P).T], axis=1)
    d["f1_b2"] = np.concatenate([i["L1_ffn_eb2"], i["L1_ffn_sh_b2"][None]], axis=0)
    d["f1_router"], d["f1_rb"] = i["L1_ffn_gate_w"], rep(i["L1_ffn_gate_b"])
    d["f3_w1"] = i["L3_ffn_w1"].transpose(1, 0, 2).reshape(P, -1)
    d["f3_w2"] = chunks(i["L3_ffn_w2"])
    d["f3_b1"], d["f3_b2"] = i["L3_ffn_b1"].reshape(32, P).T, i["L3_ffn_b2"]
    d["f3_router"], d["f3_rb"] = i["L3_ffn_wr"].T, np.zeros((P, 8), f)
    return {n: np.ascontiguousarray(a) for n, a in d.items()}


def decoder(nc, d, out):
    k = Core()
    with ExitStack() as ctx:
        sb = lambda name, shape, dt=F32: ctx.enter_context(nc.sbuf_tensor(name, shape, dt))
        k.x = sb("x", [P, NT, P])
        k.mats = sb("mats", [P, len(MATS), P])
        k.cols = sb("cols", [P, len(COLS)])
        k.rows = sb("rows", [P, len(ROWS), P])
        k.ident = sb("ident", [P, P])
        k.neghalf = sb("neghalf", [P, 32])
        k.f0w = sb("f0w", [P, 6 * 1024])
        k.moe = sb("moe", [P, 2 * 9 * 512])
        k.f0_in, k.f1_in, k.f3_in = (ctx.enter_context(nc.semaphore(n)) for n in ("f0_in", "f1_in", "f3_in"))
        k.mat = lambda n: k.mats[:, MATS.index(n), :]
        k.col = lambda n: k.cols[:, COLS.index(n):COLS.index(n) + 1]
        k.row = lambda n: k.rows[:, ROWS.index(n), :]
        load_all(nc, k, d)
        phases = {
            0: lambda: attention(nc, k, d, "a0", "a0_q", "a0_k", "a0_v", "a0_o", width=16, diff=0.8 - 0.6 * 2.718281828459045 ** (-3.6)),
            3: lambda: attention(nc, k, d, "a1", "a1_q", "a1_k", "a1_v", "a1_o", qb="a1_bq", kb="a1_bk", vb="a1_bv", ob="a1_bo"),
            7: lambda: attention(nc, k, d, "x2", "x2_q", "x2_k", "x2_v", "x2_o", kv="ctx", qb="x2_bq", kb="x2_bk", vb="x2_bv", ob="x2_bo"),
            9: lambda: attention(nc, k, d, "a3", "a3_q", "a3_k", "a3_v", "a3_o", qb="a3_bq", kb="a3_bk", vb="a3_bv", ob="a3_bo",
                                 affine=("a3_ga", "a3_be"), bias=True),
            10: lambda: attention(nc, k, d, "x3", "x3_q", "x3_k", "x3_v", kv="ctx", qb="x3_bq", kb="x3_bk", vb="x3_bv",
                                  restricted=True),
        }
        phases[1] = lambda: warping(nc, k, d, "w0")
        phases[2] = lambda: trees(nc, k, d, "f0")
        phases[4] = lambda: memory_attention(nc, k, d, "x1")
        phases[5] = lambda: experts(nc, k, d, "f1", shared=True)
        phases[6] = lambda: pooling(nc, k, d, "a2")
        phases[8] = lambda: ternary(nc, k, d, "f2")
        phases[11] = lambda: experts(nc, k, d, "f3", shared=False)
        for n in PHASES:
            phases[n]()
        store_out(nc, k, out)


def store_out(nc, k, out):
    ph = Phase(nc, "store")
    stored = ph.counter("stored")
    with nc.Block() as block:
        @block.sync
        def _(sp):
            sp.dma_start(out.rearrange("(t p) d -> p t d", p=P), k.x[:, :, :]).then_inc(stored.sem, 16)
            sp.wait_ge(stored.sem, 16)
    ph.close()


PHASES = range(12)


def kernel(**inputs):
    import numpy as np
    import concourse.bacc as bacc
    from concourse.bass_utils import run_bass_kernel_spmd

    nc = bacc.Bacc("TRN2", target_bir_lowering=False, num_devices=1)
    arrays = {f"in_{n}": a for n, a in lay_out(inputs).items()}
    d = {n[3:]: nc.dram_tensor(n, a.shape, mybir.dt.from_np(a.dtype), kind="ExternalInput").ap() for n, a in arrays.items()}
    out = nc.dram_tensor("out", (NB * SL, P), F32, kind="ExternalOutput").ap()
    decoder(nc, d, out)
    r = run_bass_kernel_spmd(nc, [arrays], core_ids=[0])
    return r.results[0]["out"].reshape(NB, SL, P)
```
